# Optimizing a Trainium2 kernel written in Bass

```python
import numpy as np
import jax
import jax.numpy as jnp

def _softmax(x, axis=-1):
    return jax.nn.softmax(x, axis=axis)

def _gelu(x):
    return jax.nn.gelu(x, approximate=True)

def _silu(x):
    return jax.nn.silu(x)

def _sigmoid(x):
    return jax.nn.sigmoid(x)

def _layernorm(x, axis=-1, eps=1e-05):
    m = jnp.mean(x, axis=axis, keepdims=True)
    v = jnp.var(x, axis=axis, keepdims=True)
    return (x - m) / jnp.sqrt(v + eps)

def _scatter_add(tgt, idx, src, axis=0):
    return tgt.at[idx].add(src)

def _segment_sum(src, seg, n):
    return jax.ops.segment_sum(src, seg, n)
kernel_name = 'mk_adj_preln_d4_adj_r2_61ffff'

def setup_inputs(seed: int=0):
    np.random.seed(seed)
    _w = jnp.asarray

    def _rec_inputs():
        import jax
        import jax.numpy as jnp
        _gk = jax.random.key(seed)
        x = -0.000929 + 1 * jax.random.normal(jax.random.fold_in(_gk, 1), (2048, 128), jnp.float32)
        _a = jax.random.bernoulli(jax.random.fold_in(_gk, 2), 0.0078125, (2048, 2048))
        adj = _a.astype(jnp.int32)
        return (x, adj)
    x, adj = _rec_inputs()

    def _L0_gnn_setup():
        import jax, jax.numpy as jnp
        import numpy as np
        N, F_IN, NHID, NHEADS, OUTDIM = (2048, 128, 128, 8, 128)
        ALPHA = 0.2
        NEG = -9000000000000000.0

        def _gat(x, adj, W_heads, a1, a2, W_out, b_out):
            Wh = jnp.einsum('nf,hfd->hnd', x, W_heads)
            s1 = jnp.einsum('hnd,hd->hn', Wh, a1)
            s2 = jnp.einsum('hnd,hd->hn', Wh, a2)
            e = s1[:, :, None] + s2[:, None, :]
            e = jnp.where(e > 0, e, ALPHA * e)
            e = jnp.where(adj[None, :, :] > 0, e, NEG)
            att = jax.nn.softmax(e, axis=-1)
            hp = jnp.einsum('hnm,hmd->hnd', att, Wh)
            hp = jax.nn.elu(hp)
            feat = jnp.transpose(hp, (1, 0, 2)).reshape(N, NHEADS * NHID)
            return feat @ W_out + b_out
        key = jax.random.key(seed)
        ks = jax.random.split(key, 7)
        x = jax.random.normal(ks[0], (N, F_IN), jnp.float32)
        adj = jax.random.randint(ks[1], (N, N), 0, 2, jnp.int32)
        W_heads = jax.random.normal(ks[2], (NHEADS, F_IN, NHID), jnp.float32) * (1.414 / np.sqrt(F_IN))
        a1 = jax.random.normal(ks[3], (NHEADS, NHID), jnp.float32) * 0.1
        a2 = jax.random.normal(ks[4], (NHEADS, NHID), jnp.float32) * 0.1
        W_out = jax.random.normal(ks[5], (NHID * NHEADS, OUTDIM), jnp.float32) * (1.0 / np.sqrt(NHID * NHEADS))
        b_out = jnp.zeros((OUTDIM,), jnp.float32)
        return {'x': x, 'adj': adj, 'W_heads': W_heads, 'a1': a1, 'a2': a2, 'W_out': W_out, 'b_out': b_out}
    _L0_gnn_all = _L0_gnn_setup()
    _L0_gnn_in = {k: v for k, v in _L0_gnn_all.items() if k in ('W_heads', 'a1', 'a2', 'W_out', 'b_out')}
    del _L0_gnn_all

    def _L1_gnn_setup():
        import jax, jax.numpy as jnp
        import numpy as np
        N_NODES = 4096
        IN_F = 128
        OUT_F = 128
        ALPHA = 0.2
        key = jax.random.key(seed)
        k1, k2, k3, k4 = jax.random.split(key, 4)
        X = jax.random.normal(k1, (N_NODES, IN_F), dtype=jnp.float32)
        A = jax.random.randint(k2, (N_NODES, N_NODES), 0, 2, dtype=jnp.int32)
        W = jax.random.normal(k3, (OUT_F, IN_F), dtype=jnp.float32) * (1.0 / np.sqrt(IN_F))
        r = jax.random.normal(k4, (2 * OUT_F, 1), dtype=jnp.float32)
        return {'X': X, 'A': A, 'W': W, 'r': r}
    _L1_gnn_all = _L1_gnn_setup()
    _L1_gnn_in = {k: v for k, v in _L1_gnn_all.items() if k in ('W', 'r')}
    del _L1_gnn_all

    def _L2_gnn_setup():
        import jax, jax.numpy as jnp
        import numpy as np
        N = 4096
        IN_F = 128
        OUT_F = 128
        ALPHA = 0.2
        NEG_INF = -1000000000000.0

        def _xavier(key, shape, gain=1.414):
            fan_in, fan_out = (shape[0], shape[1])
            bound = gain * np.sqrt(6.0 / (fan_in + fan_out))
            return jax.random.uniform(key, shape, jnp.float32, -bound, bound)
        key = jax.random.key(seed)
        k1, k2, k3, k4 = jax.random.split(key, 4)
        inp = jax.random.normal(k1, (N, IN_F), jnp.float32)
        adj = jax.random.randint(k2, (N, N), 0, 2, jnp.int32)
        W = _xavier(k3, (IN_F, OUT_F))
        a = _xavier(k4, (2 * OUT_F, 1))
        return {'inp': inp, 'adj': adj, 'W': W, 'a': a}
    _L2_gnn_all = _L2_gnn_setup()
    _L2_gnn_in = {k: v for k, v in _L2_gnn_all.items() if k in ('W', 'a')}
    del _L2_gnn_all

    def _L3_gnn_setup():
        import jax, jax.numpy as jnp
        import numpy as np
        ALPHA = 0.2
        NEG_INF = -9000000000000000.0
        key = jax.random.key(seed)
        k1, k2, k3, k4 = jax.random.split(key, 4)
        N, F_in, F_out = (4096, 128, 128)
        x = jax.random.normal(k1, (N, F_in), dtype=jnp.float32)
        adj = jax.random.randint(k2, (N, N), 0, 2, dtype=jnp.int32)
        W = jax.random.normal(k3, (F_in, F_out), dtype=jnp.float32) * (1.0 / np.sqrt(F_in))
        a = jax.random.normal(k4, (2 * F_out, 1), dtype=jnp.float32) * 0.05
        return {'x': x, 'adj': adj, 'W': W, 'a': a}
    _L3_gnn_all = _L3_gnn_setup()
    _L3_gnn_in = {k: v for k, v in _L3_gnn_all.items() if k in ('W', 'a')}
    del _L3_gnn_all
    return {'x': x, 'adj': adj, 'L0_gnn_W_heads': _L0_gnn_in['W_heads'], 'L0_gnn_a1': _L0_gnn_in['a1'], 'L0_gnn_a2': _L0_gnn_in['a2'], 'L0_gnn_W_out': _L0_gnn_in['W_out'], 'L0_gnn_b_out': _L0_gnn_in['b_out'], 'L1_gnn_W': _L1_gnn_in['W'], 'L1_gnn_r': _L1_gnn_in['r'], 'L2_gnn_W': _L2_gnn_in['W'], 'L2_gnn_a': _L2_gnn_in['a'], 'L3_gnn_W': _L3_gnn_in['W'], 'L3_gnn_a': _L3_gnn_in['a']}

def reference(x, adj, L0_gnn_W_heads, L0_gnn_a1, L0_gnn_a2, L0_gnn_W_out, L0_gnn_b_out, L1_gnn_W, L1_gnn_r, L2_gnn_W, L2_gnn_a, L3_gnn_W, L3_gnn_a):
    import jax
    import jax.numpy as jnp

    def _L0_gnn_ref(x, adj, W_heads, a1, a2, W_out, b_out):
        import jax, jax.numpy as jnp
        import numpy as np
        N, F_IN, NHID, NHEADS, OUTDIM = (2048, 128, 128, 8, 128)
        ALPHA = 0.2
        NEG = -9000000000000000.0

        def _gat(x, adj, W_heads, a1, a2, W_out, b_out):
            Wh = jnp.einsum('nf,hfd->hnd', x, W_heads)
            s1 = jnp.einsum('hnd,hd->hn', Wh, a1)
            s2 = jnp.einsum('hnd,hd->hn', Wh, a2)
            e = s1[:, :, None] + s2[:, None, :]
            e = jnp.where(e > 0, e, ALPHA * e)
            e = jnp.where(adj[None, :, :] > 0, e, NEG)
            att = jax.nn.softmax(e, axis=-1)
            hp = jnp.einsum('hnm,hmd->hnd', att, Wh)
            hp = jax.nn.elu(hp)
            feat = jnp.transpose(hp, (1, 0, 2)).reshape(N, NHEADS * NHID)
            return feat @ W_out + b_out
        return _gat(x, adj, W_heads, a1, a2, W_out, b_out)

    def _L1_gnn_ref(X, A, W, r):
        import jax, jax.numpy as jnp
        import numpy as np
        N_NODES = 4096
        IN_F = 128
        OUT_F = 128
        ALPHA = 0.2
        Wh = X @ W.T
        F_out = Wh.shape[-1]
        r_src = r[:F_out, 0]
        r_dst = r[F_out:, 0]
        s_i = Wh @ r_src
        s_j = Wh @ r_dst
        e = s_i[:, None] + s_j[None, :]
        e = jnp.where(e >= 0, e, ALPHA * e)
        e = jnp.where(A == 0, -jnp.inf, e)
        attention = jax.nn.softmax(e, axis=1)
        output = attention @ Wh
        return jax.nn.gelu(output, approximate=False)

    def _L2_gnn_ref(inp, adj, W, a):
        import jax, jax.numpy as jnp
        import numpy as np
        N = 4096
        IN_F = 128
        OUT_F = 128
        ALPHA = 0.2
        NEG_INF = -1000000000000.0

        def _xavier(key, shape, gain=1.414):
            fan_in, fan_out = (shape[0], shape[1])
            bound = gain * np.sqrt(6.0 / (fan_in + fan_out))
            return jax.random.uniform(key, shape, jnp.float32, -bound, bound)
        h = inp @ W
        a1 = a[:OUT_F, 0]
        a2 = a[OUT_F:, 0]
        s1 = h @ a1
        s2 = h @ a2
        e = jax.nn.leaky_relu(s1[:, None] + s2[None, :], negative_slope=ALPHA)
        att = jnp.where(adj > 0, e, NEG_INF)
        att = jax.nn.softmax(att, axis=1)
        h_prime = att @ h
        return jax.nn.elu(h_prime)

    def _L3_gnn_ref(x, adj, W, a):
        import jax, jax.numpy as jnp
        import numpy as np
        ALPHA = 0.2
        NEG_INF = -9000000000000000.0
        h = x @ W
        F_out = h.shape[1]
        a1 = a[:F_out, 0]
        a2 = a[F_out:, 0]
        s1 = h @ a1
        s2 = h @ a2
        e = jax.nn.leaky_relu(s1[:, None] + s2[None, :], negative_slope=ALPHA)
        scores = jnp.where(adj > 0, e, NEG_INF)
        attention = jax.nn.softmax(scores, axis=1)
        h_prime = attention @ h
        return jax.nn.elu(h_prime)
    h = jnp.maximum(_layernorm(x, axis=-1), 0.0)
    x = x + _L0_gnn_ref(h, adj, L0_gnn_W_heads, L0_gnn_a1, L0_gnn_a2, L0_gnn_W_out, L0_gnn_b_out)
    h = jnp.maximum(_layernorm(x, axis=-1), 0.0)
    x = x + _L1_gnn_ref(h, adj, L1_gnn_W, L1_gnn_r)
    h = jnp.maximum(_layernorm(x, axis=-1), 0.0)
    x = x + _L2_gnn_ref(h, adj, L2_gnn_W, L2_gnn_a)
    h = jnp.maximum(_layernorm(x, axis=-1), 0.0)
    x = x + _L3_gnn_ref(h, adj, L3_gnn_W, L3_gnn_a)
    return x

_drawn_inputs = setup_inputs


def setup_inputs(seed=0):
    import zlib

    import numpy as np

    out = dict(_drawn_inputs(seed))
    spreads = {'L0_gnn_b_out': (0.0, 0.1)}
    factors = {'L3_gnn_a': 3.9}
    for name, (base, spread) in spreads.items():
        noise = np.random.default_rng([zlib.crc32(name.encode()), seed]).standard_normal(out[name].shape)
        drawn = base * np.exp(spread * noise) if base else spread * noise
        out[name] = jnp.asarray(drawn.astype(out[name].dtype))
    for name, factor in factors.items():
        out[name] = (out[name] * factor).astype(out[name].dtype)
    return out
```

```python
import concourse.bass as bass
from concourse import mybir
from contextlib import ExitStack



def gat_stack(nc, x, adj_t, w0, a1, a2, w_out, b_out, w1_t, r1, w2, av2, w3, av3, out):
    fp32, bf16, i32 = mybir.dt.float32, mybir.dt.bfloat16, mybir.dt.int32
    ALU, ACT, AX = mybir.AluOpType, mybir.ActivationFunctionType, mybir.AxisListType

    N, D = x.shape
    H = w0.shape[0]
    P = 128
    NT = N // P
    CH = N // 2
    NK = CH // P
    VW = D + 1
    RING = 8
    PER_BANK = 512 // VW
    NB = -(-NK // PER_BANK)
    STAGE = 5
    T_AT, DEN_AT = 6, 7
    PER_LATE = 38
    ALPHA, EPS = 0.2, 1e-5
    U1, U2 = 2 * H, 2 * H + 2

    ctx = ExitStack()
    with ctx:
        def sb(name, shape, dt=fp32):
            return ctx.enter_context(nc.sbuf_tensor(name, shape, dt))

        def sem(name):
            return ctx.enter_context(nc.semaphore(name))

        adjT = sb("adjT", [P, NT, N], bf16)
        stage = sb("stage", [P, STAGE, CH], i32)
        probs = sb("probs", [P, RING, CH])
        rho = sb("rho", [P, N])
        rho_rows = sb("rho_rows", [H, N])
        V = sb("V", [P, NT, VW])
        X = sb("X", [P, NT, D])
        hT = sb("hT", [P, N])
        rows = sb("rows", [P, 2, NK, D])
        xn = sb("xn", [P, NK, D])
        fill = sb("fill", [P, NK, D])
        hpT = sb("hpT", [P, NK, P])
        W0 = sb("W0", [P, H, D])
        Wout = sb("Wout", [P, H, D])
        WL = sb("WL", [P, 3, D])
        a_rep = sb("a_rep", [P, 2, H * D])
        al_rep = sb("al_rep", [P, 3, 2, D])
        wa0 = sb("wa0", [P, 2, H])
        waL = sb("waL", [P, 4, 2])
        wa_now = sb("wa_now", [P, 2])
        bias_rep = sb("bias_rep", [P, D])
        mean_w = sb("mean_w", [P, H * D])
        mean_now = sb("mean_now", [P, D])
        ident = sb("ident", [P, P])
        stats = sb("stats", [P, NK, 6])
        mv = sb("mv", [P, NK, 2])
        nwt = sb("nwt", [P, 4, NK])
        seed = sb("seed", [P, NK], i32)
        hsum = sb("hsum", [P, 4])
        hmean = sb("hmean", [P, 2])
        cmax = sb("cmax", [P, H])
        c_row = sb("c_row", [H, 1])
        c_rep = sb("c_rep", [P, H])
        d_all = sb("d_all", [P, H, NT])
        t_all = sb("t_all", [P, H, NT])
        v_all = sb("v_all", [P, H, NT])
        t_now = sb("t_now", [P, NT])
        v_now = sb("v_now", [P, NT])
        den = sb("den", [P, 4, NK])
        rho_dram = nc.dram_tensor("rho_dram", (H, N), fp32, kind="Internal").ap()

        acc = ctx.enter_context(nc.psum_tensor("acc", [P, 2, NB, 512], fp32))
        side = ctx.enter_context(nc.psum_tensor("side", [P, 2, 512], fp32))
        score_bank = acc[:, 0, 2, :]
        s1_banks = [acc[:, 0, 0, :], acc[:, 0, 1, :], acc[:, 1, 0, :], acc[:, 1, 1, :]]

        x_in = [sem(f"x_in{c}") for c in range(2)]
        w0_in = sem("w0_in")
        w_in = sem("w_in")
        adj_in = [sem(f"adj_in{s}") for s in range(STAGE)]
        ident_zero = sem("ident_zero")
        ident_ready = sem("ident_ready")
        adj_ready = sem("adj_ready")
        wa_ready = sem("wa_ready")
        dve_step = sem("dve_step")
        norm_ready = sem("norm_ready")
        hT_psum = sem("hT_psum")
        hT_ready = sem("hT_ready")
        s2_psum = sem("s2_psum")
        cmax_ready = sem("cmax_ready")
        cmaxT_psum = sem("cmaxT_psum")
        c_row_ready = sem("c_row_ready")
        c_psum = sem("c_psum")
        d_ready = sem("d_ready")
        tv_ready = sem("tv_ready")
        s1_psum = sem("s1_psum")
        r_ready = sem("r_ready")
        rho_ready = sem("rho_ready")
        rho_stored = sem("rho_stored")
        rho_in = [sem(f"rho_in{c}") for c in range(2)]
        hmean_ready = sem("hmean_ready")
        meanw_psum = sem("meanw_psum")
        meanw_ready = sem("meanw_ready")
        mean_now_ready = sem("mean_now_ready")
        wh_psum = sem("wh_psum")
        v_ready = sem("v_ready")
        probs_ready = sem("probs_ready")
        summed = sem("summed")
        rden_ready = sem("rden_ready")
        fill_ready = sem("fill_ready")
        rows_ready = sem("rows_ready")
        out_ready = sem("out_ready")
        act_ready = sem("act_ready")
        elu_ready = sem("elu_ready")
        hpT_psum = sem("hpT_psum")
        hpT_ready = sem("hpT_ready")
        proj_psum = sem("proj_psum")
        x_added = sem("x_added")
        out_done = sem("out_done")

        block = ctx.enter_context(nc.Block())
        x_v = x.rearrange("(t p) d -> p t d", p=P)
        out_v = out.rearrange("(t p) d -> p t d", p=P)

        def group(c, k):
            return acc[:, c, k // PER_BANK, (k % PER_BANK) * VW:(k % PER_BANK) * VW + VW]

        @block.sync
        def _(sp):
            for c in range(2):
                sp.dma_start(X[:, c * NK:(c + 1) * NK, :], x_v[:, c * NK:(c + 1) * NK, :]).then_inc(x_in[c], 16)
            sp.dma_start(W0[:, :, :], w0.rearrange("h f d -> f h d")).then_inc(w0_in, 16)
            for s, a in enumerate((a1, a2)):
                sp.dma_start(a_rep[:, s, :], a.rearrange("(o h) d -> o (h d)", o=1).to_broadcast([P, H * D])).then_inc(w0_in, 16)
            for n in range(2 * NT):
                c, j = n // NT, n % NT
                if n >= STAGE:
                    sp.wait_ge(adj_ready, n - STAGE + 1)
                sp.dma_start(stage[:, n % STAGE, :], adj_t[j * P:(j + 1) * P, c * CH:(c + 1) * CH]).then_inc(adj_in[n % STAGE], 16)
            sp.wait_ge(out_ready, 1)
            sp.dma_start(out_v[:, 0:NK, :], X[:, 0:NK, :]).then_inc(out_done, 16)
            sp.wait_ge(out_ready, 2)
            sp.dma_start(out_v[:, NK:NT, :], X[:, NK:NT, :]).then_inc(out_done, 16)
            sp.wait_ge(out_done, 32)

        @block.gpsimd
        def _(pool):
            nc.gpsimd.memset(ident[:, :], 0.0).then_inc(ident_zero, 1)
            pool.wait_ge(ident_zero, 1)
            nc.gpsimd.affine_select(out=ident[:, :], in_=ident[:, :], compare_op=ALU.not_equal, fill=1.0,
                                    base=0, pattern=[[-1, P]], channel_multiplier=1).then_inc(ident_ready, 1)
            for l, w in enumerate((w1_t, w2, w3)):
                pool.dma_start(WL[:, l, :], w).then_inc(w_in, 16)
            for l, a in enumerate((r1, av2, av3)):
                pool.dma_start(al_rep[:, l, :, :].rearrange("p s d -> p (s d)"),
                               a.rearrange("k o -> o k").to_broadcast([P, 2 * D])).then_inc(w_in, 16)
            pool.dma_start(bias_rep[:, :], b_out.rearrange("(o d) -> o d", o=1).to_broadcast([P, D])).then_inc(w_in, 16)
            pool.dma_start(Wout[:, :, :], w_out.rearrange("(h d) o -> d h o", h=H)).then_inc(w_in, 16)

            def load_rho(h, c):
                pool.dma_start(rho[:, c * CH:(c + 1) * CH],
                               rho_dram[bass.ds(h, 1), c * CH:(c + 1) * CH].to_broadcast([P, CH])).then_inc(rho_in[c], 16)

            for c in range(2):
                pool.wait_ge(rho_ready, 2 * c + 2)
                pool.dma_start(rho_dram[:, c * CH:(c + 1) * CH], rho_rows[:, c * CH:(c + 1) * CH]).then_inc(rho_stored, 16)
                pool.wait_ge(rho_stored, 16 * c + 16)
                load_rho(0, c)
            with pool.Fori(0, H - 1) as h:
                for c in range(2):
                    pool.wait_ge(probs_ready, h * (2 * NT) + (c + 1) * NT)
                    load_rho(h + 1, c)

        @block.tensor
        def _(pe):
            def early_scores(n, c, heads, wa_s1, wa_s2):
                for r in range(2 * c, 2 * c + 2):
                    pe.wait_ge(norm_ready, n * 4 + r + 1)
                    for k in range(4):
                        last = nc.tensor.transpose(side[:, r % 2, k * P:(k + 1) * P],
                                                   xn[:, (r % 2) * 4 + k, :], ident[:, :])
                    last.then_inc(hT_psum, 1)
                pe.wait_ge(hT_ready, n * 4 + 2 * c + 2)
                if c == 0:
                    pe.wait_ge(wa_ready, n + 1)
                for j in range(c * NK, (c + 1) * NK):
                    last = nc.tensor.matmul(score_bank[:, j * heads:(j + 1) * heads], hT[:, j * P:(j + 1) * P],
                                            wa_s2, start=True, stop=True)
                last.then_inc(s2_psum, 1)

            def s1(k, wa_s1):
                nc.tensor.matmul(s1_banks[k][0:wa_s1.shape[1], :], wa_s1, hT[:, k * 512:(k + 1) * 512],
                                 start=True, stop=True).then_inc(s1_psum, 1)

            def late_scores(n, heads, wa_s1):
                pe.wait_ge(cmax_ready, n + 1)
                nc.tensor.transpose(score_bank[0:heads, 256:256 + P], cmax[:, 0:heads], ident[:, :]).then_inc(cmaxT_psum, 1)
                s1(2, wa_s1)
                pe.wait_ge(c_row_ready, n + 1)
                nc.tensor.matmul(score_bank[:, 384:384 + heads], c_row[0:heads, 0:1].to_broadcast([heads, P]),
                                 ident[0:heads, 0:heads], start=True, stop=True).then_inc(c_psum, 1)
                s1(3, wa_s1)

            def project(q, w, before=None):
                for g in range(4):
                    if g >= 2:
                        pe.wait_ge(v_ready, q * 4 + g - 1)
                    elif before is not None:
                        pe.wait_ge(x_added, before)
                    for k in range(4):
                        j = 4 * g + k
                        last = nc.tensor.matmul(side[:, g % 2, k * D:(k + 1) * D], hT[:, j * P:(j + 1) * P], w,
                                                start=True, stop=True)
                    last.then_inc(wh_psum, 1)

            def mean_rows(m, q, w, heads):
                pe.wait_ge(hmean_ready, m)
                pe.wait_ge(v_ready, q * 4 + 4)
                cols = min(512, heads * D)
                for k in range(heads * D // cols):
                    last = nc.tensor.matmul(side[:, k, 0:cols], hmean[:, 1:2].to_broadcast([P, P]),
                                            w[:, k * cols:(k + 1) * cols], start=True, stop=True)
                last.then_inc(meanw_psum, 1)

            def unit(u, c, q, asides=()):
                for j in range(NT):
                    if j == 0 and not (isinstance(u, int) and u == 0):
                        pe.wait_ge(rows_ready, 2 * u - 1)
                    if c == 0 and j % 4 == 0:
                        pe.wait_ge(v_ready, q * 4 + j // 4 + 1)
                    pe.wait_ge(probs_ready, u * NT + j + 1)
                    for k in range(NK):
                        last = nc.tensor.matmul(group(c, k), probs[:, j % RING, k * P:(k + 1) * P], V[:, j, :],
                                                start=(j == 0 and k % PER_BANK == 0), stop=(j == NT - 1),
                                                skip_group_check=True)
                    last.then_inc(summed, 1)
                    for at, work in asides:
                        if at == j:
                            work()

            def transpose_rows(u, q):
                pe.wait_ge(elu_ready, u + 1)
                pe.wait_ge(x_added, 2 * u + 1)
                pe.wait_ge(v_ready, q * 4 + 4)
                for b in range(2):
                    for k in range(4):
                        last = nc.tensor.transpose(side[:, b, k * P:(k + 1) * P], rows[:, 0, 4 * b + k, :], ident[:, :])
                    last.then_inc(hpT_psum, 1)

            def out_projection(u, w):
                for b in range(2):
                    pe.wait_ge(hpT_ready, 2 * u + b + 1)
                    for k in range(4):
                        last = nc.tensor.matmul(side[:, b, k * D:(k + 1) * D], hpT[:, 4 * b + k, :], w,
                                                start=True, stop=True)
                    last.then_inc(proj_psum, 1)

            def aside(u, q, w):
                return ((T_AT, lambda: transpose_rows(u, q)), (T_AT + 2, lambda: out_projection(u, w)))

            def head_of(t, h):
                return t[:, bass.ds(h, 1), :].rearrange("p a d -> p (a d)")

            pe.wait_ge(ident_ready, 1)
            wa1, wa2 = wa0[:, 0, :], wa0[:, 1, :]
            for c in range(2):
                early_scores(0, c, H, wa1, wa2)
                if c == 0:
                    s1(0, wa1)
                    s1(1, wa1)
            late_scores(0, H, wa1)
            project(0, W0[:, 0, :])
            unit(0, 0, 0, ((5, lambda: mean_rows(1, 0, W0[:, :, :].rearrange("p h d -> p (h d)"), H)),))
            pe.wait_ge(meanw_ready, 1)
            pe.wait_ge(w_in, 8 * 16)
            with pe.Fori(0, H - 1) as h:
                unit(2 * h + 1, 1, h, aside(2 * h, h, head_of(Wout, h)))
                project(h + 1, head_of(W0, h + 1), before=4 * h + 3)
                unit(2 * h + 2, 0, h + 1, aside(2 * h + 1, h + 1, head_of(Wout, h)))
            unit(2 * H - 1, 1, H - 1, aside(2 * H - 2, H - 1, Wout[:, H - 1, :]))

            wa1, wa2 = wa_now[:, 0:1].to_broadcast([P, P]), wa_now[:, 1:2]
            pe.wait_ge(x_added, 4 * H - 1)
            early_scores(1, 0, 1, wa1, wa2)
            s1(0, wa1)
            s1(1, wa1)
            transpose_rows(2 * H - 1, H - 1)
            out_projection(2 * H - 1, Wout[:, H - 1, :])
            early_scores(1, 1, 1, wa1, wa2)
            late_scores(1, 1, wa1)
            project(H, WL[:, 0, :])
            unit(U1, 0, H)
            unit(U1 + 1, 1, H)
            early_scores(2, 0, 1, wa1, wa2)
            s1(0, wa1)
            s1(1, wa1)
            with pe.Fori(0, 2) as l:
                w = head_of(WL, l + 1)
                early_scores(l + 2, 1, 1, wa1, wa2)
                late_scores(l + 2, 1, wa1)
                project(l + (H + 1), w)
                unit(2 * l + U2, 0, l + (H + 1), ((5, lambda: mean_rows(l + 2, l + (H + 1), w, 1)),))
                unit(2 * l + (U2 + 1), 1, l + (H + 1))
                pe.wait_ge(meanw_ready, l + 2)
                early_scores(l + 3, 0, 1, wa1, wa2)
                s1(0, wa1)
                s1(1, wa1)

        @block.scalar
        def _(act):
            def cast(n0, n1):
                for n in range(n0, n1):
                    c, j = n // NT, n % NT
                    act.wait_ge(adj_in[n % STAGE], 16 * (n // STAGE + 1))
                    nc.scalar.activation(adjT[:, j, c * CH:(c + 1) * CH], stage[:, n % STAGE, :], ACT.Sign).then_inc(adj_ready, 1)

            def relu_transposed(n, c):
                for r in range(2 * c, 2 * c + 2):
                    act.wait_ge(hT_psum, n * 4 + r + 1)
                    nc.scalar.activation(hT[:, r * 512:(r + 1) * 512], side[:, r % 2, :], ACT.Relu,
                                         accum_out=hsum[:, r:r + 1]).then_inc(hT_ready, 1)

            def factors(n, heads):
                act.wait_ge(d_ready, n + 1)
                t_out = t_all[:, :, :] if heads > 1 else t_now[:, :]
                v_out = v_all[:, :, :] if heads > 1 else v_now[:, :]
                d_in = d_all[:, :, :] if heads > 1 else d_all[:, 0, :]
                nc.scalar.activation(t_out, d_in, ACT.Exp, scale=1 - ALPHA).then_inc(tv_ready, 1)
                nc.scalar.activation(v_out, d_in, ACT.Exp, scale=ALPHA).then_inc(tv_ready, 1)

            def rho_exp(n, c, heads):
                r_buf = rho_rows if heads > 1 else rho
                for k in range(2 * c, 2 * c + 2):
                    act.wait_ge(r_ready, n * 4 + k + 1)
                    nc.scalar.activation(r_buf[:, k * 512:(k + 1) * 512], r_buf[:, k * 512:(k + 1) * 512], ACT.Exp,
                                         scale=-(1 - ALPHA)).then_inc(rho_ready, 1)

            def scale_v(q, between=None):
                for g in range(4):
                    act.wait_ge(wh_psum, q * 4 + g + 1)
                    if g == 0:
                        nc.scalar.activation(V[:, :, D], v_now[:, :], ACT.Copy)
                    for k in range(4):
                        last = nc.scalar.activation(V[:, 4 * g + k, 0:D], side[:, g % 2, k * D:(k + 1) * D], ACT.Copy,
                                                    scale=v_now[:, 4 * g + k:4 * g + k + 1])
                    last.then_inc(v_ready, 1)
                    if between is not None:
                        between(g)

            def copy_mean(m, heads):
                act.wait_ge(meanw_psum, m)
                cols = min(512, heads * D)
                for k in range(heads * D // cols):
                    last = nc.scalar.activation(mean_w[:, k * cols:(k + 1) * cols], side[:, k, 0:cols], ACT.Copy)
                last.then_inc(meanw_ready, 1)
                act.wait_ge(meanw_ready, m)

            def take_mean(w, count):
                nc.scalar.activation(mean_now[:, :], w, ACT.Copy).then_inc(mean_now_ready, 1)
                act.wait_ge(mean_now_ready, count)

            def fill_rows(u, f):
                act.wait_ge(rden_ready, u + 1)
                for k in range(NK):
                    ins = nc.scalar.activation(fill[:, k, :], mean_now[:, :], ACT.Copy, scale=den[:, 1, k:k + 1])
                    if k % 4 == 3:
                        ins.then_inc(fill_ready, 1)

            def nonlinear(u, func):
                for b in range(2):
                    act.wait_ge(rows_ready, 2 * u + b + 2)
                    nc.scalar.activation(rows[:, 1, 4 * b:4 * b + 4, :], rows[:, 0, 4 * b:4 * b + 4, :],
                                         func).then_inc(act_ready, 1)

            def copy_transposed(u):
                for b in range(2):
                    act.wait_ge(hpT_psum, 2 * u + b + 1)
                    nc.scalar.activation(hpT[:, 4 * b:4 * b + 4, :], side[:, b, :].rearrange("p (k i) -> p k i", k=4),
                                         ACT.Copy).then_inc(hpT_ready, 1)

            def finish(u):
                fill_rows(u, u)
                nonlinear(u, ACT.Exp)
                copy_transposed(u)

            relu_transposed(0, 0)
            cast(0, 2)
            relu_transposed(0, 1)
            cast(2, 6)
            factors(0, H)
            rho_exp(0, 0, H)
            act.wait_ge(tv_ready, 2)
            nc.scalar.activation(v_now[:, :], v_all[:, 0, :], ACT.Copy).then_inc(tv_ready, 1)
            act.wait_ge(tv_ready, 3)
            rho_exp(0, 1, H)
            scale_v(0, lambda g: cast(6 + 3 * g, 9 + 3 * g))
            copy_mean(1, H)
            take_mean(mean_w[:, 0:D], 1)
            cast(18, 2 * NT)
            with act.Fori(0, H - 1) as h:
                finish(2 * h)
                nc.scalar.activation(v_now[:, :], v_all[:, bass.ds(h + 1, 1), :].rearrange("p a t -> p (a t)"),
                                     ACT.Copy).then_inc(tv_ready, 1)
                act.wait_ge(tv_ready, h + 4)
                scale_v(h + 1)
                finish(2 * h + 1)
                take_mean(mean_w[:, bass.ds((h + 1) * D, D)], h + 2)
            finish(2 * H - 2)
            relu_transposed(1, 0)
            finish(2 * H - 1)

            relu_transposed(1, 1)
            factors(1, 1)
            rho_exp(1, 0, 1)
            act.wait_ge(tv_ready, H + 4)
            scale_v(H)
            rho_exp(1, 1, 1)
            nonlinear(U1, ACT.Gelu)
            relu_transposed(2, 0)
            nonlinear(U1 + 1, ACT.Gelu)
            with act.Fori(0, 2) as l:
                relu_transposed(l + 2, 1)
                factors(l + 2, 1)
                rho_exp(l + 2, 0, 1)
                act.wait_ge(tv_ready, 2 * l + (H + 6))
                scale_v(l + (H + 1))
                rho_exp(l + 2, 1, 1)
                copy_mean(l + 2, 1)
                take_mean(mean_w[:, 0:D], l + (H + 1))
                for c in range(2):
                    fill_rows(2 * l + (U2 + c), 2 * l + (2 * H + c))
                    nonlinear(2 * l + (U2 + c), ACT.Exp)
                    if c == 0:
                        relu_transposed(l + 3, 0)

        @block.vector
        def _(dve):
            steps = [0]
            base = [0]

            def link(ins):
                steps[0] += 1
                ins.then_inc(dve_step, 1)
                dve.wait_ge(dve_step, base[0] + steps[0])

            def norm(n, c):
                for k in range(NK):
                    last = nc.vector.bn_stats(stats[:, k, :], X[:, c * NK + k, :])
                link(last)
                nc.vector.memset(nwt[:, 2, :], 0.0)
                for k in range(NK):
                    last = nc.vector.bn_aggr(mv[:, k, :], stats[:, k, :])
                link(last)
                y, v, s = nwt[:, 0, :], nwt[:, 1, :], nwt[:, 2, :]
                link(nc.vector.tensor_scalar(v, mv[:, :, 1], EPS, None, ALU.add))
                link(nc.vector.tensor_scalar(seed[:, :], v.bitcast(i32), -0.5, 1597463007.0, ALU.mult, ALU.add))
                g = seed[:, :].bitcast(fp32)
                for it in range(3):
                    link(nc.vector.scalar_tensor_tensor(s, g, -0.5, g, ALU.mult, ALU.mult))
                    link(nc.vector.tensor_tensor(s, s, v, ALU.mult))
                    link(nc.vector.scalar_tensor_tensor(y, s, 1.5, g, ALU.add, ALU.mult))
                    g = y
                if c == 1 or not isinstance(n, int) or n > 0:
                    dve.wait_ge(hT_psum, n * 4 + 2 * c)
                for k in range(NK):
                    ins = nc.vector.tensor_scalar(xn[:, k, :], X[:, c * NK + k, :], mv[:, k, 0:1], y[:, k:k + 1],
                                                  ALU.subtract, ALU.mult)
                    if k % 4 == 3:
                        ins.then_inc(norm_ready, 1)

            def center(n, heads):
                dve.wait_ge(s2_psum, 2 * n + 2)
                s2 = score_bank[:, 0:NT * heads].rearrange("p (t h) -> p h t", h=heads)
                nc.vector.tensor_reduce(cmax[:, 0:heads], s2, AX.X, ALU.max).then_inc(cmax_ready, 1)
                dve.wait_ge(cmaxT_psum, n + 1)
                nc.vector.tensor_reduce(c_row[0:heads, :], score_bank[0:heads, 256:256 + P], AX.X, ALU.max).then_inc(c_row_ready, 1)
                dve.wait_ge(c_psum, n + 1)
                link(nc.vector.tensor_copy(c_rep[:, 0:heads], score_bank[:, 384:384 + heads]))
                for k in range(heads):
                    last = nc.vector.tensor_scalar(d_all[:, k, :], s2[:, k, :], c_rep[:, k:k + 1], None, ALU.subtract)
                last.then_inc(d_ready, 1)

            def mean(n, m):
                dve.wait_ge(hT_ready, n * 4 + 4)
                link(nc.vector.tensor_reduce(hmean[:, 0:1], hsum[:, :], AX.X, ALU.add))
                nc.vector.tensor_scalar(hmean[:, 1:2], hmean[:, 0:1], 1.0 / N, None, ALU.mult).then_inc(hmean_ready, 1)

            def r_rows(n, c, heads):
                r_buf, c_s, m = (rho_rows, c_row, heads) if heads > 1 else (rho, c_rep, P)
                for k in range(2 * c, 2 * c + 2):
                    dve.wait_ge(s1_psum, n * 4 + k + 1)
                    nc.vector.tensor_scalar(r_buf[0:m, k * 512:(k + 1) * 512], s1_banks[k][0:m, :], c_s[0:m, 0:1], 0.0,
                                            ALU.add, ALU.max).then_inc(r_ready, 1)

            def unit(u, c, before=None, asides=()):
                for j in range(NT):
                    if before is not None:
                        before(j)
                    if not (isinstance(u, int) and u * NT + j < RING):
                        dve.wait_ge(summed, u * NT + j - RING + 1)
                    nc.vector.scalar_tensor_tensor(probs[:, j % RING, :], rho[:, c * CH:(c + 1) * CH], t_now[:, j:j + 1],
                                                   adjT[:, j, c * CH:(c + 1) * CH], ALU.max, ALU.mult).then_inc(probs_ready, 1)
                    for at, work in asides:
                        if at == j:
                            work()

            def denominators(u, c, empties=True):
                dve.wait_ge(summed, (u + 1) * NT)
                full = NK // PER_BANK
                nc.vector.tensor_copy(den[:, 0, 0:full * PER_BANK].rearrange("p (b g) -> p b g", g=PER_BANK),
                                      acc[:, c, 0:full, D:D + PER_BANK * VW - D:VW])
                link(nc.vector.tensor_copy(den[:, 0, full * PER_BANK:NK],
                                           acc[:, c, full, D:D + (NK - full * PER_BANK - 1) * VW + 1:VW]))
                if empties:
                    nc.vector.tensor_scalar(den[:, 1, :], den[:, 0, :], 0.0, None, ALU.is_equal)
                    link(nc.vector.scalar_tensor_tensor(den[:, 2, :], den[:, 0, :], 0.0, den[:, 0, :], ALU.is_equal, ALU.add))
                nc.vector.reciprocal(den[:, 3, :], den[:, 2 if empties else 0, :]).then_inc(rden_ready, 1)
                dve.wait_ge(rden_ready, u + 1)

            def divide(u, c, f):
                for k in range(NK):
                    if f is not None:
                        if k % 4 == 0:
                            dve.wait_ge(fill_ready, 2 * f + k // 4 + 1)
                        ins = nc.vector.scalar_tensor_tensor(rows[:, 0, k, :], group(c, k)[:, 0:D], den[:, 3, k:k + 1],
                                                             fill[:, k, :], ALU.mult, ALU.add)
                    else:
                        ins = nc.vector.tensor_scalar(rows[:, 0, k, :], group(c, k)[:, 0:D], den[:, 3, k:k + 1], None, ALU.mult)
                    if k % 4 == 3:
                        ins.then_inc(rows_ready, 1)

            def elu(u):
                dve.wait_ge(act_ready, 2 * u + 2)
                link(nc.vector.tensor_scalar(rows[:, 1, :, :], rows[:, 1, :, :], 1.0, 1.0, ALU.min, ALU.subtract))
                nc.vector.scalar_tensor_tensor(rows[:, 0, :, :], rows[:, 0, :, :], 0.0, rows[:, 1, :, :],
                                               ALU.max, ALU.add).then_inc(elu_ready, 1)

            def add_projection(u, c):
                for b in range(2):
                    dve.wait_ge(proj_psum, 2 * u + b + 1)
                    at = X[:, c * NK + 4 * b:c * NK + 4 * b + 4, :]
                    nc.vector.tensor_tensor(at, at, side[:, b, :].rearrange("p (k d) -> p k d", k=4), ALU.add).then_inc(x_added, 1)

            def head0_asides(u, c):
                return ((DEN_AT, lambda: denominators(u, c)),
                        (DEN_AT + 2, lambda: divide(u, c, u)),
                        (DEN_AT + 4, lambda: elu(u)),
                        (15, lambda: add_projection(u, c)))

            def add_elu(u, c):
                for b in range(2):
                    at = X[:, c * NK + 4 * b:c * NK + 4 * b + 4, :]
                    dve.wait_ge(rows_ready, 2 * u + b + 2)
                    last = nc.vector.scalar_tensor_tensor(at, rows[:, 0, 4 * b:4 * b + 4, :], 0.0, at, ALU.max, ALU.add)
                link(last)
                for b in range(2):
                    dve.wait_ge(act_ready, 2 * u + b + 1)
                    e = rows[:, 1, 4 * b:4 * b + 4, :]
                    last = nc.vector.tensor_scalar(e, e, 1.0, 1.0, ALU.min, ALU.subtract)
                link(last)
                at = X[:, c * NK:(c + 1) * NK, :]
                link(nc.vector.tensor_tensor(at, at, rows[:, 1, :, :], ALU.add))

            def add_gelu(u, c):
                for b in range(2):
                    at = X[:, c * NK + 4 * b:c * NK + 4 * b + 4, :]
                    dve.wait_ge(act_ready, 2 * u + b + 1)
                    last = nc.vector.tensor_tensor(at, at, rows[:, 1, 4 * b:4 * b + 4, :], ALU.add)
                link(last)

            dve.wait_ge(x_in[0], 16)
            norm(0, 0)
            dve.wait_ge(w0_in, 48)
            for s in range(2):
                link(nc.vector.tensor_tensor(a_rep[:, s, :], W0[:, :, :].rearrange("p h d -> p (h d)"), a_rep[:, s, :], ALU.mult))
                last = nc.vector.tensor_reduce(wa0[:, s, :], a_rep[:, s, :].rearrange("p (h d) -> p h d", h=H), AX.X, ALU.add)
            last.then_inc(wa_ready, 1)
            dve.wait_ge(x_in[1], 16)
            norm(0, 1)
            center(0, H)
            r_rows(0, 0, H)
            r_rows(0, 1, H)
            dve.wait_ge(tv_ready, 1)
            nc.vector.tensor_copy(t_now[:, :], t_all[:, 0, :]).then_inc(rows_ready, 1)
            dve.wait_ge(rows_ready, 1)
            mean(0, 1)

            def rho_and_adj(h, c, blocks):
                def before(j):
                    if j == 0:
                        dve.wait_ge(rho_in[c], (h + 1) * 16)
                    if blocks:
                        dve.wait_ge(adj_ready, c * NT + j + 1)
                return before

            def attention_vectors():
                dve.wait_ge(w_in, 8 * 16)
                for s in range(2):
                    link(nc.vector.tensor_tensor(al_rep[:, :, s, :], al_rep[:, :, s, :], WL[:, :, :], ALU.mult))
                nc.vector.memset(waL[:, 3, :], 0.0)
                link(nc.vector.tensor_reduce(waL[:, 0:3, :], al_rep[:, :, :, :], AX.X, ALU.add))
                nc.vector.tensor_tensor(X[:, :, :], X[:, :, :], bias_rep[:, :].rearrange("p (a d) -> p a d", a=1)
                                        .to_broadcast([P, NT, D]), ALU.add).then_inc(x_added, 1)
                dve.wait_ge(x_added, 1)

            unit(0, 0, rho_and_adj(0, 0, True), ((8, attention_vectors),))
            PER = 1 + 2 * 3
            outside, steps[0] = steps[0], 0
            with dve.Fori(0, H - 1) as h:
                base[0] = h * PER + outside
                unit(2 * h + 1, 1, rho_and_adj(h, 1, True), head0_asides(2 * h, 0))
                dve.wait_ge(probs_ready, (2 * h + 2) * NT)
                link(nc.vector.tensor_copy(t_now[:, :], t_all[:, bass.ds(h + 1, 1), :].rearrange("p a t -> p (a t)")))
                unit(2 * h + 2, 0, rho_and_adj(h + 1, 0, False), head0_asides(2 * h + 1, 1))
                assert steps[0] == PER
            base[0] = 0
            steps[0] = outside + (H - 1) * PER
            unit(2 * H - 1, 1, rho_and_adj(H - 1, 1, False), head0_asides(2 * H - 2, 0))
            nc.vector.tensor_copy(wa_now[:, :], waL[:, 0, :]).then_inc(wa_ready, 1)
            dve.wait_ge(x_added, 4 * H - 1)
            norm(1, 0)
            for _, work in head0_asides(2 * H - 1, 1):
                work()
            dve.wait_ge(x_added, 4 * H + 1)
            norm(1, 1)

            center(1, 1)
            r_rows(1, 0, 1)
            dve.wait_ge(tv_ready, H + 3)
            dve.wait_ge(rho_ready, 6)
            unit(U1, 0, None, ((5, lambda: r_rows(1, 1, 1)),))
            dve.wait_ge(rho_ready, 8)

            def next_attention_vectors(n, l):
                dve.wait_ge(s1_psum, n * 4 + 4)
                nc.vector.tensor_copy(wa_now[:, :], waL[:, bass.ds(l, 1), :].rearrange("p a s -> p (a s)")
                                      if not isinstance(l, int) else waL[:, l, :]).then_inc(wa_ready, 1)

            unit(U1 + 1, 1, None, ((DEN_AT, lambda: denominators(U1, 0, False)),
                                   (DEN_AT + 1, lambda: divide(U1, 0, None)),
                                   (DEN_AT + 4, lambda: add_gelu(U1, 0)),
                                   (15, lambda: (next_attention_vectors(1, 1), norm(2, 0)))))
            denominators(U1 + 1, 1, False)
            divide(U1 + 1, 1, None)
            add_gelu(U1 + 1, 1)

            PER = PER_LATE
            outside, steps[0] = steps[0], 0
            with dve.Fori(0, 2) as l:
                base[0] = l * PER + outside
                n, u, f = l + 2, 2 * l + U2, 2 * l + 2 * H
                norm(n, 1)
                center(n, 1)
                r_rows(n, 0, 1)
                dve.wait_ge(tv_ready, 2 * l + (H + 5))
                dve.wait_ge(rho_ready, 4 * l + 10)
                mean(n, n)
                unit(u, 0, None, ((5, lambda: r_rows(n, 1, 1)),))
                dve.wait_ge(rho_ready, 4 * l + 12)

                unit(u + 1, 1, None, ((DEN_AT, lambda: denominators(u, 0)),
                                      (DEN_AT + 2, lambda: divide(u, 0, f)),
                                      (DEN_AT + 4, lambda: add_elu(u, 0)),
                                      (15, lambda: (next_attention_vectors(n, l + 2), norm(n + 1, 0)))))
                denominators(u + 1, 1)
                divide(u + 1, 1, f + 1)
                add_elu(u + 1, 1)
                print("links", steps[0])
                assert steps[0] == PER
            for k in range(2):
                nc.vector.memset(hmean[:, k:k + 1], 0.0).then_inc(out_ready, 1)


_INS = ["x", "adj_t", "L0_gnn_W_heads", "L0_gnn_a1", "L0_gnn_a2", "L0_gnn_W_out", "L0_gnn_b_out", "L1_gnn_W_t",
        "L1_gnn_r", "L2_gnn_W", "L2_gnn_a", "L3_gnn_W", "L3_gnn_a"]


def kernel(**inputs):
    import numpy as _np
    import concourse.bacc as _bacc
    from concourse import mybir as _mybir
    from concourse.bass_utils import run_bass_kernel_spmd as _run

    laid = dict(inputs)
    laid["adj_t"] = _np.asarray(inputs["adj"]).T
    laid["L1_gnn_W_t"] = _np.asarray(inputs["L1_gnn_W"]).T
    nc = _bacc.Bacc("TRN2", target_bir_lowering=False, num_devices=1)
    arrays, args = {}, []
    for name in _INS:
        a = _np.ascontiguousarray(laid[name])
        arrays[f"in_{name}_dram"] = a
        args.append(nc.dram_tensor(f"in_{name}_dram", a.shape, _mybir.dt.from_np(a.dtype), kind="ExternalInput").ap())
    out = nc.dram_tensor("out_0_dram", inputs["x"].shape, _mybir.dt.float32, kind="ExternalOutput").ap()
    gat_stack(nc, *args, out)
    r = _run(nc, [arrays], core_ids=[0])
    return r.results[0]["out_0_dram"]
```

```python
import concourse.bass as bass
from concourse import mybir
from contextlib import ExitStack



def gat_stack(nc, x, adj_t, w0, w0_t, a0, w_out, b_out, w1_t, w1, r1, w2, w2_t, av2, w3, w3_t, av3, out):
    fp32, bf16, i32 = mybir.dt.float32, mybir.dt.bfloat16, mybir.dt.int32
    ALU, ACT, AX = mybir.AluOpType, mybir.ActivationFunctionType, mybir.AxisListType

    N, D = x.shape
    H = w0.shape[0]
    P = 128
    NT = N // P
    CH = N // 2
    NK = CH // P
    VW = D + 1
    RING = 8
    PER_BANK = 512 // VW
    NB = -(-NK // PER_BANK)
    STAGE = 5
    T_AT, DEN_AT = 8, 7
    PER_LATE = 41
    ALPHA, EPS = 0.2, 1e-5
    U1, U2 = 2 * H, 2 * H + 2

    ctx = ExitStack()
    with ctx:
        def sb(name, shape, dt=fp32):
            return ctx.enter_context(nc.sbuf_tensor(name, shape, dt))

        def sem(name):
            return ctx.enter_context(nc.semaphore(name))

        adjT = sb("adjT", [P, NT, N], bf16)
        stage = sb("stage", [P, STAGE, CH], i32)
        probs = sb("probs", [P, RING, CH])
        rho = sb("rho", [P, N])
        rho_rows = sb("rho_rows", [H, N])
        V = sb("V", [P, NT, VW])
        X = sb("X", [P, NT, D])
        hT = sb("hT", [P, N])
        rows = sb("rows", [P, 2, NK, D])
        xn = sb("xn", [P, NK, D])
        fill = sb("fill", [P, NK, D])
        hpT = sb("hpT", [P, NK, P])
        W0 = sb("W0", [P, H, D])
        Wout = sb("Wout", [P, H, D])
        WL = sb("WL", [P, 4, VW])
        W0t = sb("W0t", [P, H, D])
        WLt = sb("WLt", [P, 3, D])
        a0_sb = sb("a0_sb", [P, H, 2])
        aL_sb = sb("aL_sb", [P, 3, 2])
        wa0 = sb("wa0", [P, 2, H])
        waL = sb("waL", [P, 4, 2])
        wa_now = sb("wa_now", [P, 2])
        bias_rep = sb("bias_rep", [P, D])
        mean_w = sb("mean_w", [P, H * D])
        mean_now = sb("mean_now", [P, D])
        ident = sb("ident", [P, P])
        stats = sb("stats", [P, NT, 6])
        mv = sb("mv", [P, NT, 2])
        nwt = sb("nwt", [P, 4, NT])
        seed = sb("seed", [P, NT], i32)
        hsum = sb("hsum", [P, 4])
        hmean = sb("hmean", [P, 2])
        cmax = sb("cmax", [P, H])
        s2_col = sb("s2_col", [P, NT])
        c_row = sb("c_row", [H, 1])
        c_rep = sb("c_rep", [P, H])
        d_all = sb("d_all", [P, H, NT])
        t_all = sb("t_all", [P, H, NT])
        v_all = sb("v_all", [P, H, NT])
        t_now = sb("t_now", [P, NT])
        v_now = sb("v_now", [P, NT])
        den = sb("den", [P, 4, NK])
        empty = sb("empty", [P, 2, NK])
        rho_dram = nc.dram_tensor("rho_dram", (H, N), fp32, kind="Internal").ap()

        acc = ctx.enter_context(nc.psum_tensor("acc", [P, 2, NB, 512], fp32))
        side = ctx.enter_context(nc.psum_tensor("side", [P, 2, 512], fp32))
        score_bank = acc[:, 0, 2, :]
        CT, CC, CW = 260, 390, 480
        s1_banks = [acc[:, 0, 0, :], acc[:, 0, 1, :], acc[:, 1, 0, :], acc[:, 1, 1, :]]

        x_in = [sem(f"x_in{c}") for c in range(2)]
        w0_in = sem("w0_in")
        w0t_in = sem("w0t_in")
        w_in = sem("w_in")
        adj_in = [sem(f"adj_in{s}") for s in range(STAGE)]
        ident_zero = sem("ident_zero")
        ident_ready = sem("ident_ready")
        adj_ready = sem("adj_ready")
        wa_ready = sem("wa_ready")
        dve_step = sem("dve_step")
        wa_psum = sem("wa_psum")
        waL_psum = sem("waL_psum")
        waL_ready = sem("waL_ready")
        rstd_ready = sem("rstd_ready")
        norm_dve = sem("norm_dve")
        norm_act = sem("norm_act")
        hT_psum = sem("hT_psum")
        hT_ready = sem("hT_ready")
        s2_psum = sem("s2_psum")
        cmax_ready = sem("cmax_ready")
        cmaxT_psum = sem("cmaxT_psum")
        c_row_ready = sem("c_row_ready")
        c_psum = sem("c_psum")
        d_ready = sem("d_ready")
        tv_ready = sem("tv_ready")
        s1_psum = sem("s1_psum")
        r_ready = sem("r_ready")
        rho_ready = sem("rho_ready")
        rho_stored = sem("rho_stored")
        rho_in = [sem(f"rho_in{c}") for c in range(2)]
        hmean_ready = sem("hmean_ready")
        meanw_psum = sem("meanw_psum")
        meanw_ready = sem("meanw_ready")
        mean_now_ready = sem("mean_now_ready")
        wh_psum = sem("wh_psum")
        v_ready = sem("v_ready")
        probs_ready = sem("probs_ready")
        summed = sem("summed")
        rden_ready = sem("rden_ready")
        fill_ready = sem("fill_ready")
        rows_ready = sem("rows_ready")
        out_ready = sem("out_ready")
        act_ready = sem("act_ready")
        elu_ready = sem("elu_ready")
        hpT_psum = sem("hpT_psum")
        hpT_ready = sem("hpT_ready")
        proj_psum = sem("proj_psum")
        x_added = sem("x_added")
        out_done = sem("out_done")

        block = ctx.enter_context(nc.Block())
        x_v = x.rearrange("(t p) d -> p t d", p=P)
        out_v = out.rearrange("(t p) d -> p t d", p=P)

        def group(c, k):
            return acc[:, c, k // PER_BANK, (k % PER_BANK) * VW:(k % PER_BANK) * VW + VW]

        def first_norm(n):
            return isinstance(n, int) and n == 0

        @block.sync
        def _(sp):
            for c in range(2):
                sp.dma_start(X[:, c * NK:(c + 1) * NK, :], x_v[:, c * NK:(c + 1) * NK, :]).then_inc(x_in[c], 16)
            sp.dma_start(W0t[:, :, :], w0_t.rearrange("h d f -> d h f")).then_inc(w0t_in, 16)
            sp.dma_start(a0_sb[:, :, :], a0).then_inc(w0t_in, 16)
            sp.dma_start(W0[:, :, :], w0.rearrange("h f d -> f h d")).then_inc(w0_in, 16)
            for n in range(2 * NT):
                c, j = n // NT, n % NT
                if n >= STAGE:
                    sp.wait_ge(adj_ready, n - STAGE + 1)
                sp.dma_start(stage[:, n % STAGE, :], adj_t[j * P:(j + 1) * P, c * CH:(c + 1) * CH]).then_inc(adj_in[n % STAGE], 16)
            sp.wait_ge(out_ready, 1)
            sp.dma_start(out_v[:, 0:NK, :], X[:, 0:NK, :]).then_inc(out_done, 16)
            sp.wait_ge(out_ready, 2)
            sp.dma_start(out_v[:, NK:NT, :], X[:, NK:NT, :]).then_inc(out_done, 16)
            sp.wait_ge(out_done, 32)

        @block.gpsimd
        def _(pool):
            nc.gpsimd.memset(ident[:, :], 0.0).then_inc(ident_zero, 1)
            pool.wait_ge(ident_zero, 1)
            nc.gpsimd.affine_select(out=ident[:, :], in_=ident[:, :], compare_op=ALU.not_equal, fill=1.0,
                                    base=0, pattern=[[-1, P]], channel_multiplier=1).then_inc(ident_ready, 1)
            for l, w in enumerate((w1_t, w2, w3)):
                pool.dma_start(WL[:, l, 0:D], w).then_inc(w_in, 16)
            for l, w in enumerate((w1, w2_t, w3_t)):
                pool.dma_start(WLt[:, l, :], w).then_inc(w_in, 16)
            for l, a in enumerate((r1, av2, av3)):
                pool.dma_start(aL_sb[:, l, :], a).then_inc(w_in, 16)
            pool.dma_start(bias_rep[:, :], b_out.rearrange("(o d) -> o d", o=1).to_broadcast([P, D])).then_inc(w_in, 16)
            pool.dma_start(Wout[:, :, :], w_out.rearrange("(h d) o -> d h o", h=H)).then_inc(w_in, 16)

            def load_rho(h, c):
                pool.dma_start(rho[:, c * CH:(c + 1) * CH],
                               rho_dram[bass.ds(h, 1), c * CH:(c + 1) * CH].to_broadcast([P, CH])).then_inc(rho_in[c], 16)

            for c in range(2):
                pool.wait_ge(rho_ready, 2 * c + 2)
                pool.dma_start(rho_dram[:, c * CH:(c + 1) * CH], rho_rows[:, c * CH:(c + 1) * CH]).then_inc(rho_stored, 16)
                pool.wait_ge(rho_stored, 16 * c + 16)
                load_rho(0, c)
            with pool.Fori(0, H - 1) as h:
                for c in range(2):
                    pool.wait_ge(probs_ready, h * (2 * NT) + (c + 1) * NT)
                    load_rho(h + 1, c)

        @block.tensor
        def _(pe):
            def transpose_normed(n, c):
                for r in range(2 * c, 2 * c + 2):
                    pe.wait_ge(norm_act if r % 2 else norm_dve, 2 * n + c + 1)
                    for k in range(4):
                        last = nc.tensor.transpose(side[:, r % 2, k * P:(k + 1) * P],
                                                   xn[:, (r % 2) * 4 + k, :], ident[:, :])
                    last.then_inc(hT_psum, 1)
                pe.wait_ge(hT_ready, n * 4 + 2 * c + 2)
                if c == 0:
                    pe.wait_ge(wa_ready, n + 1)

            def s2_of_heads(c):
                for j in range(c * NK, (c + 1) * NK):
                    last = nc.tensor.matmul(score_bank[:, j * H:(j + 1) * H], hT[:, j * P:(j + 1) * P],
                                            wa0[:, 1, :], start=True, stop=True)
                last.then_inc(s2_psum, 1)

            def wh_and_s2(c, w):
                for k in range(NK):
                    at = (c * NK + k) * P
                    last = nc.tensor.matmul(group(c, k), hT[:, at:at + P], w, start=True, stop=True)
                last.then_inc(s2_psum, 1)

            def s1(k, wa_s1, bank):
                nc.tensor.matmul(bank[0:wa_s1.shape[1], :], wa_s1, hT[:, k * 512:(k + 1) * 512],
                                 start=True, stop=True).then_inc(s1_psum, 1)

            def project(q, g, w, before=None):
                if g >= 2:
                    pe.wait_ge(v_ready, q * 4 + g - 1)
                elif before is not None:
                    pe.wait_ge(x_added, before + g)
                for k in range(4):
                    j = 4 * g + k
                    last = nc.tensor.matmul(side[:, g % 2, k * D:(k + 1) * D], hT[:, j * P:(j + 1) * P], w,
                                            start=True, stop=True)
                last.then_inc(wh_psum, 1)

            def spread_max(n, heads, meanwhile):
                pe.wait_ge(cmax_ready, n + 1)
                nc.tensor.transpose(score_bank[0:heads, CT:CT + P], cmax[:, 0:heads], ident[:, :]).then_inc(cmaxT_psum, 1)
                meanwhile()
                pe.wait_ge(c_row_ready, n + 1)
                nc.tensor.matmul(score_bank[:, CC:CC + heads], c_row[0:heads, 0:1].to_broadcast([heads, P]),
                                 ident[0:heads, 0:heads], start=True, stop=True).then_inc(c_psum, 1)

            def late_scores(n, wa_s1, w):
                transpose_normed(n, 1)
                wh_and_s2(1, w)
                spread_max(n, 1, lambda: s1(0, wa_s1, side[:, 0, :]))
                s1(1, wa_s1, side[:, 1, :])
                for k in (2, 3):
                    pe.wait_ge(r_ready, n * 4 + k - 1)
                    s1(k, wa_s1, side[:, k - 2, :])

            def rest_of_wh(q, w):
                return ((1, lambda: project(q, 2, w)), (3, lambda: project(q, 3, w)))

            def mean_rows(m, w, heads, sem_free, value):
                pe.wait_ge(hmean_ready, m)
                pe.wait_ge(sem_free, value)
                cols = min(512, heads * D)
                for k in range(heads * D // cols):
                    last = nc.tensor.matmul(side[:, k, 0:cols], hmean[:, 1:2].to_broadcast([P, P]),
                                            w[:, k * cols:(k + 1) * cols], start=True, stop=True)
                last.then_inc(meanw_psum, 1)

            def unit(u, c, q, asides=(), later=False):
                for j in range(NT):
                    if j == 0 and not (isinstance(u, int) and u == 0):
                        pe.wait_ge(rows_ready, 2 * u - 1)
                    if c == 0 and j % 4 == 0:
                        pe.wait_ge(v_ready, q * 4 + max(j // 4 + 1, 2 if later else 1))
                    pe.wait_ge(probs_ready, u * NT + j + 1)
                    for k in range(NK):
                        last = nc.tensor.matmul(group(c, k), probs[:, j % RING, k * P:(k + 1) * P], V[:, j, :],
                                                start=(j == 0 and k % PER_BANK == 0), stop=(j == NT - 1),
                                                skip_group_check=True)
                    last.then_inc(summed, 1)
                    for at, work in asides:
                        if at == j:
                            work()

            def transpose_rows(u, q):
                pe.wait_ge(elu_ready, u + 1)
                pe.wait_ge(x_added, 2 * u + 1)
                pe.wait_ge(v_ready, q * 4 + 4)
                for b in range(2):
                    for k in range(4):
                        last = nc.tensor.transpose(side[:, b, k * P:(k + 1) * P], rows[:, 0, 4 * b + k, :], ident[:, :])
                    last.then_inc(hpT_psum, 1)

            def out_projection(u, w):
                for b in range(2):
                    pe.wait_ge(hpT_ready, 2 * u + b + 1)
                    for k in range(4):
                        last = nc.tensor.matmul(side[:, b, k * D:(k + 1) * D], hpT[:, 4 * b + k, :], w,
                                                start=True, stop=True)
                    last.then_inc(proj_psum, 1)

            def aside(u, q, w):
                return ((T_AT, lambda: transpose_rows(u, q)), (T_AT + 2, lambda: out_projection(u, w)))

            def head_of(t, h):
                return t[:, bass.ds(h, 1), :].rearrange("p a d -> p (a d)")

            pe.wait_ge(w0t_in, 32)
            for h in range(H):
                last = nc.tensor.matmul(score_bank[:, CW + 2 * h:CW + 2 * h + 2], W0t[:, h, :], a0_sb[:, h, :],
                                        start=True, stop=True)
            last.then_inc(wa_psum, 1)

            def later_vectors():
                pe.wait_ge(w_in, 11 * 16)
                pe.wait_ge(meanw_ready, 1)
                for l in range(3):
                    last = nc.tensor.matmul(side[:, 0, 2 * l:2 * l + 2], WLt[:, l, :], aL_sb[:, l, :], start=True, stop=True)
                last.then_inc(waL_psum, 1)

            pe.wait_ge(ident_ready, 1)
            wa1 = wa0[:, 0, :]
            for c in range(2):
                transpose_normed(0, c)
                s2_of_heads(c)
            spread_max(0, H, lambda: s1(0, wa1, s1_banks[0]))
            s1(1, wa1, s1_banks[1])
            pe.wait_ge(w0_in, 16)
            project(0, 0, W0[:, 0, :])
            project(0, 1, W0[:, 0, :])
            s1(2, wa1, s1_banks[2])
            s1(3, wa1, s1_banks[3])
            unit(0, 0, 0, rest_of_wh(0, W0[:, 0, :]) + (
                (7, lambda: mean_rows(1, W0[:, :, :].rearrange("p h d -> p (h d)"), H, v_ready, 4)),
                (13, later_vectors)))
            pe.wait_ge(waL_ready, 1)
            with pe.Fori(0, H - 1) as h:
                w = head_of(W0, h + 1)
                unit(2 * h + 1, 1, h, aside(2 * h, h, head_of(Wout, h)) + (
                    (11, lambda: project(h + 1, 0, w, before=4 * h + 2)),
                    (12, lambda: project(h + 1, 1, w, before=4 * h + 2)),
                    (14, lambda: project(h + 1, 2, w))))
                project(h + 1, 3, w)
                unit(2 * h + 2, 0, h + 1, aside(2 * h + 1, h + 1, head_of(Wout, h)))
            unit(2 * H - 1, 1, H - 1, aside(2 * H - 2, H - 1, Wout[:, H - 1, :]))

            wa1 = wa_now[:, 0:1].to_broadcast([P, P])
            pe.wait_ge(x_added, 4 * H - 1)
            transpose_normed(1, 0)
            wh_and_s2(0, WL[:, 0, :])
            transpose_rows(2 * H - 1, H - 1)
            out_projection(2 * H - 1, Wout[:, H - 1, :])
            late_scores(1, wa1, WL[:, 0, :])
            unit(U1, 0, H, later=True)
            unit(U1 + 1, 1, H)
            transpose_normed(2, 0)
            wh_and_s2(0, WL[:, 1, :])
            with pe.Fori(0, 2) as l:
                w = head_of(WL, l + 1)
                late_scores(l + 2, wa1, w)
                unit(2 * l + U2, 0, l + (H + 1), ((7, lambda: mean_rows(l + 2, w[:, 0:D], 1, r_ready, l * 4 + 12)),),
                     later=True)
                unit(2 * l + (U2 + 1), 1, l + (H + 1))
                pe.wait_ge(meanw_ready, l + 2)
                transpose_normed(l + 3, 0)
                wh_and_s2(0, head_of(WL, l + 2))

        @block.scalar
        def _(act):
            def cast(n0, n1):
                for n in range(n0, n1):
                    c, j = n // NT, n % NT
                    act.wait_ge(adj_in[n % STAGE], 16 * (n // STAGE + 1))
                    nc.scalar.activation(adjT[:, j, c * CH:(c + 1) * CH], stage[:, n % STAGE, :], ACT.Sign).then_inc(adj_ready, 1)

            def relu_transposed(n, c):
                act.wait_ge(rstd_ready, n + 1 if first_norm(n) else 2 * n + c)
                for k in range(4, NK):
                    at = c * NK + k
                    last = nc.scalar.activation(xn[:, k, :], X[:, at, :], ACT.Identity, bias=nwt[:, 3, at:at + 1],
                                                scale=nwt[:, 0, at:at + 1])
                last.then_inc(norm_act, 1)
                for r in range(2 * c, 2 * c + 2):
                    act.wait_ge(hT_psum, n * 4 + r + 1)
                    nc.scalar.activation(hT[:, r * 512:(r + 1) * 512], side[:, r % 2, :], ACT.Relu,
                                         accum_out=hsum[:, r:r + 1]).then_inc(hT_ready, 1)

            def factors(n, heads):
                act.wait_ge(d_ready, n + 1)
                t_out = t_all[:, :, :] if heads > 1 else t_now[:, :]
                v_out = v_all[:, :, :] if heads > 1 else v_now[:, :]
                d_in = d_all[:, :, :] if heads > 1 else d_all[:, 0, :]
                nc.scalar.activation(t_out, d_in, ACT.Exp, scale=1 - ALPHA).then_inc(tv_ready, 1)
                nc.scalar.activation(v_out, d_in, ACT.Exp, scale=ALPHA).then_inc(tv_ready, 1)

            def rho_exp(n, c, heads):
                r_buf = rho_rows if heads > 1 else rho
                for k in range(2 * c, 2 * c + 2):
                    act.wait_ge(r_ready, n * 4 + k + 1)
                    nc.scalar.activation(r_buf[:, k * 512:(k + 1) * 512], r_buf[:, k * 512:(k + 1) * 512], ACT.Exp,
                                         scale=-(1 - ALPHA)).then_inc(rho_ready, 1)

            def scale_v(q, between=None):
                for g in range(4):
                    act.wait_ge(wh_psum, q * 4 + g + 1)
                    nc.scalar.activation(V[:, 4 * g:4 * g + 4, D], v_now[:, 4 * g:4 * g + 4], ACT.Copy)
                    for k in range(4):
                        last = nc.scalar.activation(V[:, 4 * g + k, 0:D], side[:, g % 2, k * D:(k + 1) * D], ACT.Copy,
                                                    scale=v_now[:, 4 * g + k:4 * g + k + 1])
                    last.then_inc(v_ready, 1)
                    if between is not None:
                        between(g)

            def scale_v_later(c):
                nc.scalar.activation(V[:, c * NK:(c + 1) * NK, D], v_now[:, c * NK:(c + 1) * NK], ACT.Copy)
                for k in range(NK):
                    at = c * NK + k
                    ins = nc.scalar.activation(V[:, at, 0:D], group(c, k)[:, 0:D], ACT.Copy, scale=v_now[:, at:at + 1])
                    if k % 4 == 3:
                        ins.then_inc(v_ready, 1)

            def copy_mean(m, heads):
                act.wait_ge(meanw_psum, m)
                cols = min(512, heads * D)
                for k in range(heads * D // cols):
                    last = nc.scalar.activation(mean_w[:, k * cols:(k + 1) * cols], side[:, k, 0:cols], ACT.Copy)
                last.then_inc(meanw_ready, 1)
                act.wait_ge(meanw_ready, m)

            def take_mean(w, count):
                nc.scalar.activation(mean_now[:, :], w, ACT.Copy).then_inc(mean_now_ready, 1)
                act.wait_ge(mean_now_ready, count)

            def fill_rows(c):
                for k in range(NK):
                    ins = nc.scalar.activation(fill[:, k, :], mean_now[:, :], ACT.Copy, scale=empty[:, c, k:k + 1])
                    if k % 4 == 3:
                        ins.then_inc(fill_ready, 1)

            def nonlinear(u, func):
                for b in range(2):
                    act.wait_ge(rows_ready, 2 * u + b + 2)
                    nc.scalar.activation(rows[:, 1, 4 * b:4 * b + 4, :], rows[:, 0, 4 * b:4 * b + 4, :],
                                         func).then_inc(act_ready, 1)

            def copy_transposed(u):
                for b in range(2):
                    act.wait_ge(hpT_psum, 2 * u + b + 1)
                    nc.scalar.activation(hpT[:, 4 * b:4 * b + 4, :], side[:, b, :].rearrange("p (k i) -> p k i", k=4),
                                         ACT.Copy).then_inc(hpT_ready, 1)

            def finish(u, c):
                act.wait_ge(rden_ready, u + 1)
                fill_rows(c)
                nonlinear(u, ACT.Exp)
                copy_transposed(u)

            act.wait_ge(wa_psum, 1)
            nc.scalar.activation(wa0[:, :, :], score_bank[:, CW:CW + 2 * H].rearrange("p (h s) -> p s h", s=2),
                                 ACT.Copy).then_inc(wa_ready, 1)
            relu_transposed(0, 0)
            relu_transposed(0, 1)
            cast(0, 6)
            factors(0, H)
            rho_exp(0, 0, H)
            act.wait_ge(tv_ready, 2)
            nc.scalar.activation(v_now[:, :], v_all[:, 0, :], ACT.Copy).then_inc(tv_ready, 1)
            act.wait_ge(tv_ready, 3)
            rho_exp(0, 1, H)
            scale_v(0, lambda g: cast(6 + 3 * g, 9 + 3 * g))
            copy_mean(1, H)
            take_mean(mean_w[:, 0:D], 1)
            cast(18, 24)
            act.wait_ge(waL_psum, 1)
            nc.scalar.activation(WL[:, 0:3, D], side[:, 0, 1:6:2], ACT.Copy)
            nc.scalar.activation(waL[:, 0:3, :], side[:, 0, 0:6].rearrange("p (l s) -> p l s", l=3), ACT.Copy).then_inc(waL_ready, 1)
            cast(24, 2 * NT)
            with act.Fori(0, H - 1) as h:
                finish(2 * h, 0)
                nc.scalar.activation(v_now[:, :], v_all[:, bass.ds(h + 1, 1), :].rearrange("p a t -> p (a t)"),
                                     ACT.Copy).then_inc(tv_ready, 1)
                act.wait_ge(tv_ready, h + 4)
                scale_v(h + 1)
                finish(2 * h + 1, 1)
                take_mean(mean_w[:, bass.ds((h + 1) * D, D)], h + 2)
            finish(2 * H - 2, 0)
            relu_transposed(1, 0)
            finish(2 * H - 1, 1)

            relu_transposed(1, 1)
            factors(1, 1)
            rho_exp(1, 0, 1)
            act.wait_ge(tv_ready, H + 4)
            scale_v_later(0)
            scale_v_later(1)
            rho_exp(1, 1, 1)
            nonlinear(U1, ACT.Gelu)
            relu_transposed(2, 0)
            nonlinear(U1 + 1, ACT.Gelu)
            with act.Fori(0, 2) as l:
                relu_transposed(l + 2, 1)
                factors(l + 2, 1)
                rho_exp(l + 2, 0, 1)
                act.wait_ge(tv_ready, 2 * l + (H + 6))
                scale_v_later(0)
                scale_v_later(1)
                rho_exp(l + 2, 1, 1)
                copy_mean(l + 2, 1)
                take_mean(mean_w[:, 0:D], l + (H + 1))
                for c in range(2):
                    fill_rows(c)
                    nonlinear(2 * l + (U2 + c), ACT.Exp)
                    if c == 0:
                        relu_transposed(l + 3, 0)

        @block.vector
        def _(dve):
            steps = [0]
            base = [0]

            def link(ins):
                steps[0] += 1
                ins.then_inc(dve_step, 1)
                dve.wait_ge(dve_step, base[0] + steps[0])

            def mark(ins):
                steps[0] += 1
                ins.then_inc(dve_step, 1)
                return base[0] + steps[0]

            def norm(n, halves, written=(None, None)):
                first, end = halves[0] * NK, (halves[-1] + 1) * NK
                for k in range(first, end):
                    if first_norm(n) and k % NK == 0:
                        dve.wait_ge(x_in[k // NK], 16)
                    elif not first_norm(n) and k % 4 == 0:
                        dve.wait_ge(dve_step, written[k % NK // 4])
                    last = nc.vector.bn_stats(stats[:, k, :], X[:, k, :])
                link(last)
                nc.vector.memset(nwt[:, 2, first:end], 0.0)
                for k in range(first, end):
                    last = nc.vector.bn_aggr(mv[:, k, :], stats[:, k, :])
                link(last)
                y, v, s, m = (nwt[:, i, first:end] for i in range(4))
                link(nc.vector.tensor_scalar(v, mv[:, first:end, 1], EPS, None, ALU.add))
                link(nc.vector.tensor_scalar(seed[:, first:end], v.bitcast(i32), -0.5, 1597463007.0, ALU.mult, ALU.add))
                g = seed[:, first:end].bitcast(fp32)
                for it in range(3):
                    link(nc.vector.scalar_tensor_tensor(s, g, -0.5, g, ALU.mult, ALU.mult))
                    link(nc.vector.tensor_tensor(s, s, v, ALU.mult))
                    link(nc.vector.scalar_tensor_tensor(y, s, 1.5, g, ALU.add, ALU.mult))
                    g = y
                nc.vector.scalar_tensor_tensor(m, mv[:, first:end, 0], -1.0, y, ALU.mult, ALU.mult).then_inc(rstd_ready, 1)
                for c in halves:
                    if c == 1 or not first_norm(n):
                        dve.wait_ge(hT_psum, n * 4 + 2 * c)
                    for k in range(4):
                        at = c * NK + k
                        ins = nc.vector.tensor_scalar(xn[:, k, :], X[:, at, :], mv[:, at, 0:1], nwt[:, 0, at:at + 1],
                                                      ALU.subtract, ALU.mult)
                    ins.then_inc(norm_dve, 1)

            def last_columns(to, c):
                full = NK // PER_BANK
                nc.vector.tensor_copy(to[:, 0:full * PER_BANK].rearrange("p (b g) -> p b g", g=PER_BANK),
                                      acc[:, c, 0:full, D:D + PER_BANK * VW - D:VW])
                link(nc.vector.tensor_copy(to[:, full * PER_BANK:NK],
                                           acc[:, c, full, D:D + (NK - full * PER_BANK - 1) * VW + 1:VW]))

            def center(n, heads):
                dve.wait_ge(s2_psum, 2 * n + 2)
                if heads > 1:
                    s2 = score_bank[:, 0:NT * heads].rearrange("p (t h) -> p h t", h=heads)
                else:
                    for c in range(2):
                        last_columns(s2_col[:, c * NK:(c + 1) * NK], c)
                    s2 = s2_col[:, :]
                nc.vector.tensor_reduce(cmax[:, 0:heads], s2, AX.X, ALU.max).then_inc(cmax_ready, 1)
                dve.wait_ge(cmaxT_psum, n + 1)
                nc.vector.tensor_reduce(c_row[0:heads, :], score_bank[0:heads, CT:CT + P], AX.X, ALU.max).then_inc(c_row_ready, 1)
                dve.wait_ge(c_psum, n + 1)
                link(nc.vector.tensor_copy(c_rep[:, 0:heads], score_bank[:, CC:CC + heads]))
                for k in range(heads):
                    last = nc.vector.tensor_scalar(d_all[:, k, :], s2[:, k, :] if heads > 1 else s2, c_rep[:, k:k + 1],
                                                   None, ALU.subtract)
                last.then_inc(d_ready, 1)

            def mean(n, m):
                dve.wait_ge(hT_ready, n * 4 + 4)
                link(nc.vector.tensor_reduce(hmean[:, 0:1], hsum[:, :], AX.X, ALU.add))
                nc.vector.tensor_scalar(hmean[:, 1:2], hmean[:, 0:1], 1.0 / N, None, ALU.mult).then_inc(hmean_ready, 1)

            def r_rows(n, c, heads):
                r_buf, c_s, m = (rho_rows, c_row, heads) if heads > 1 else (rho, c_rep, P)
                for k in range(2 * c, 2 * c + 2):
                    dve.wait_ge(s1_psum, n * 4 + k + 1)
                    bank = s1_banks[k] if heads > 1 else side[:, k % 2, :]
                    nc.vector.tensor_scalar(r_buf[0:m, k * 512:(k + 1) * 512], bank[0:m, :], c_s[0:m, 0:1], 0.0,
                                            ALU.add, ALU.max).then_inc(r_ready, 1)

            def unit(u, c, before=None, asides=()):
                for j in range(NT):
                    if before is not None:
                        before(j)
                    if not (isinstance(u, int) and u * NT + j < RING):
                        dve.wait_ge(summed, u * NT + j - RING + 1)
                    nc.vector.scalar_tensor_tensor(probs[:, j % RING, :], rho[:, c * CH:(c + 1) * CH], t_now[:, j:j + 1],
                                                   adjT[:, j, c * CH:(c + 1) * CH], ALU.max, ALU.mult).then_inc(probs_ready, 1)
                    for at, work in asides:
                        if at == j:
                            work()

            def denominators(u, c, guard=True, store=False):
                dve.wait_ge(summed, (u + 1) * NT)
                last_columns(den[:, 0, :], c)
                if store:
                    nc.vector.tensor_scalar(empty[:, c, :], den[:, 0, :], 0.0, None, ALU.is_equal)
                if guard:
                    link(nc.vector.scalar_tensor_tensor(den[:, 2, :], den[:, 0, :], 0.0, den[:, 0, :], ALU.is_equal, ALU.add))
                nc.vector.reciprocal(den[:, 3, :], den[:, 2 if guard else 0, :]).then_inc(rden_ready, 1)
                dve.wait_ge(rden_ready, u + 1)

            def divide(u, c, f):
                for k in range(NK):
                    if f is not None:
                        if k % 4 == 0:
                            dve.wait_ge(fill_ready, 2 * f + k // 4 + 1)
                        ins = nc.vector.scalar_tensor_tensor(rows[:, 0, k, :], group(c, k)[:, 0:D], den[:, 3, k:k + 1],
                                                             fill[:, k, :], ALU.mult, ALU.add)
                    else:
                        ins = nc.vector.tensor_scalar(rows[:, 0, k, :], group(c, k)[:, 0:D], den[:, 3, k:k + 1], None, ALU.mult)
                    if k % 4 == 3:
                        ins.then_inc(rows_ready, 1)

            def elu(u):
                dve.wait_ge(act_ready, 2 * u + 2)
                link(nc.vector.tensor_scalar(rows[:, 1, :, :], rows[:, 1, :, :], 1.0, 1.0, ALU.min, ALU.subtract))
                nc.vector.scalar_tensor_tensor(rows[:, 0, :, :], rows[:, 0, :, :], 0.0, rows[:, 1, :, :],
                                               ALU.max, ALU.add).then_inc(elu_ready, 1)

            def add_projection(u, c):
                for b in range(2):
                    dve.wait_ge(proj_psum, 2 * u + b + 1)
                    at = X[:, c * NK + 4 * b:c * NK + 4 * b + 4, :]
                    nc.vector.tensor_tensor(at, at, side[:, b, :].rearrange("p (k d) -> p k d", k=4), ALU.add).then_inc(x_added, 1)

            def head0_asides(u, c):
                return ((DEN_AT, lambda: denominators(u, c, store=True)),
                        (DEN_AT + 2, lambda: divide(u, c, u)),
                        (DEN_AT + 4, lambda: elu(u)),
                        (15, lambda: add_projection(u, c)))

            def add_elu(u, c):
                at = [X[:, c * NK + 4 * b:c * NK + 4 * b + 4, :] for b in range(2)]
                for b in range(2):
                    dve.wait_ge(rows_ready, 2 * u + b + 2)
                    last = nc.vector.scalar_tensor_tensor(at[b], rows[:, 0, 4 * b:4 * b + 4, :], 0.0, at[b], ALU.max, ALU.add)
                link(last)
                written = []
                for b in range(2):
                    dve.wait_ge(act_ready, 2 * u + b + 1)
                    written.append(mark(nc.vector.scalar_tensor_tensor(at[b], rows[:, 1, 4 * b:4 * b + 4, :], 1.0, at[b],
                                                                       ALU.min, ALU.add)))
                return written

            def add_gelu(u, c):
                written = []
                for b in range(2):
                    at = X[:, c * NK + 4 * b:c * NK + 4 * b + 4, :]
                    dve.wait_ge(act_ready, 2 * u + b + 1)
                    written.append(mark(nc.vector.tensor_tensor(at, at, rows[:, 1, 4 * b:4 * b + 4, :], ALU.add)))
                return written

            kept = []

            norm(0, (0, 1))
            center(0, H)
            r_rows(0, 0, H)
            r_rows(0, 1, H)
            dve.wait_ge(tv_ready, 1)
            nc.vector.tensor_copy(t_now[:, :], t_all[:, 0, :]).then_inc(rows_ready, 1)
            dve.wait_ge(rows_ready, 1)
            mean(0, 1)

            def rho_and_adj(h, c, blocks):
                def before(j):
                    if j == 0:
                        dve.wait_ge(rho_in[c], (h + 1) * 16)
                    if blocks:
                        dve.wait_ge(adj_ready, c * NT + j + 1)
                return before

            def add_bias():
                dve.wait_ge(w_in, 11 * 16)
                nc.vector.memset(WL[:, 3, :], 0.0)
                link(nc.vector.memset(waL[:, 3, :], 0.0))
                nc.vector.tensor_tensor(X[:, :, :], X[:, :, :], bias_rep[:, :].rearrange("p (a d) -> p a d", a=1)
                                        .to_broadcast([P, NT, D]), ALU.add).then_inc(x_added, 1)
                dve.wait_ge(x_added, 1)

            unit(0, 0, rho_and_adj(0, 0, True), ((8, add_bias),))
            PER = 1 + 2 * 3
            outside, steps[0] = steps[0], 0
            with dve.Fori(0, H - 1) as h:
                base[0] = h * PER + outside
                unit(2 * h + 1, 1, rho_and_adj(h, 1, True), head0_asides(2 * h, 0))
                dve.wait_ge(probs_ready, (2 * h + 2) * NT)
                link(nc.vector.tensor_copy(t_now[:, :], t_all[:, bass.ds(h + 1, 1), :].rearrange("p a t -> p (a t)")))
                unit(2 * h + 2, 0, rho_and_adj(h + 1, 0, False), head0_asides(2 * h + 1, 1))
                assert steps[0] == PER
            base[0] = 0
            steps[0] = outside + (H - 1) * PER
            unit(2 * H - 1, 1, rho_and_adj(H - 1, 1, False), head0_asides(2 * H - 2, 0))
            dve.wait_ge(waL_ready, 1)
            nc.vector.tensor_copy(wa_now[:, :], waL[:, 0, :]).then_inc(wa_ready, 1)
            dve.wait_ge(x_added, 4 * H - 1)
            last_link = base[0] + steps[0]
            norm(1, (0,), (last_link, last_link))
            for _, work in head0_asides(2 * H - 1, 1):
                work()
            dve.wait_ge(x_added, 4 * H + 1)
            last_link = base[0] + steps[0]
            norm(1, (1,), (last_link, last_link))

            center(1, 1)
            r_rows(1, 0, 1)
            dve.wait_ge(tv_ready, H + 3)
            dve.wait_ge(rho_ready, 6)
            unit(U1, 0, None, ((5, lambda: r_rows(1, 1, 1)),))
            dve.wait_ge(rho_ready, 8)

            def next_attention_vectors(n, l):
                dve.wait_ge(s1_psum, n * 4 + 4)
                nc.vector.tensor_copy(wa_now[:, :], waL[:, bass.ds(l, 1), :].rearrange("p a s -> p (a s)")
                                      if not isinstance(l, int) else waL[:, l, :]).then_inc(wa_ready, 1)

            unit(U1 + 1, 1, None, ((DEN_AT, lambda: denominators(U1, 0, False)),
                                   (DEN_AT + 1, lambda: divide(U1, 0, None)),
                                   (DEN_AT + 4, lambda: kept.append(add_gelu(U1, 0))),
                                   (15, lambda: (next_attention_vectors(1, 1), norm(2, (0,), kept.pop())))))
            denominators(U1 + 1, 1, False)
            divide(U1 + 1, 1, None)
            norm(2, (1,), add_gelu(U1 + 1, 1))

            PER = PER_LATE
            outside, steps[0] = steps[0], 0
            with dve.Fori(0, 2) as l:
                base[0] = l * PER + outside
                n, u, f = l + 2, 2 * l + U2, 2 * l + 2 * H
                center(n, 1)
                r_rows(n, 0, 1)
                dve.wait_ge(tv_ready, 2 * l + (H + 5))
                dve.wait_ge(rho_ready, 4 * l + 10)
                mean(n, n)
                unit(u, 0, None, ((5, lambda: r_rows(n, 1, 1)),
                                  (9, lambda: link(nc.vector.tensor_scalar(X[:, :, :], X[:, :, :], 1.0, None, ALU.subtract)))))
                dve.wait_ge(rho_ready, 4 * l + 12)

                unit(u + 1, 1, None, ((DEN_AT, lambda: denominators(u, 0)),
                                      (DEN_AT + 2, lambda: divide(u, 0, f)),
                                      (DEN_AT + 4, lambda: kept.append(add_elu(u, 0))),
                                      (15, lambda: (next_attention_vectors(n, l + 2), norm(n + 1, (0,), kept.pop())))))
                denominators(u + 1, 1)
                divide(u + 1, 1, f + 1)
                norm(n + 1, (1,), add_elu(u + 1, 1))
                print("links", steps[0])
                assert steps[0] == PER
            for k in range(2):
                nc.vector.memset(hmean[:, k:k + 1], 0.0).then_inc(out_ready, 1)


_INS = ["x", "adj_t", "L0_gnn_W_heads", "W0_t", "a0", "L0_gnn_W_out", "L0_gnn_b_out", "W1_t", "L1_gnn_W", "r1",
        "L2_gnn_W", "W2_t", "a2", "L3_gnn_W", "W3_t", "a3"]


def kernel(**inputs):
    import numpy as _np
    import concourse.bacc as _bacc
    from concourse import mybir as _mybir
    from concourse.bass_utils import run_bass_kernel_spmd as _run

    laid = dict(inputs)
    laid["adj_t"] = _np.asarray(inputs["adj"]).T
    laid["W0_t"] = _np.asarray(inputs["L0_gnn_W_heads"]).transpose(0, 2, 1)
    laid["a0"] = _np.stack([_np.asarray(inputs["L0_gnn_a1"]), _np.asarray(inputs["L0_gnn_a2"])], axis=-1).transpose(1, 0, 2)
    laid["W1_t"] = _np.asarray(inputs["L1_gnn_W"]).T
    laid["W2_t"] = _np.asarray(inputs["L2_gnn_W"]).T
    laid["W3_t"] = _np.asarray(inputs["L3_gnn_W"]).T
    for to, name in (("r1", "L1_gnn_r"), ("a2", "L2_gnn_a"), ("a3", "L3_gnn_a")):
        laid[to] = _np.asarray(inputs[name]).reshape(2, -1).T
    nc = _bacc.Bacc("TRN2", target_bir_lowering=False, num_devices=1)
    arrays, args = {}, []
    for name in _INS:
        a = _np.ascontiguousarray(laid[name])
        arrays[f"in_{name}_dram"] = a
        args.append(nc.dram_tensor(f"in_{name}_dram", a.shape, _mybir.dt.from_np(a.dtype), kind="ExternalInput").ap())
    out = nc.dram_tensor("out_0_dram", inputs["x"].shape, _mybir.dt.float32, kind="ExternalOutput").ap()
    gat_stack(nc, *args, out)
    r = _run(nc, [arrays], core_ids=[0])
    return r.results[0]["out_0_dram"]
```

```python
import concourse.bass as bass
from concourse import mybir
from contextlib import ExitStack



def gat_stack(nc, x, adj_t, w0, w0_t, a0, w_out, b_out, w1_t, w1, r1, w2, w2_t, av2, w3, w3_t, av3, out):
    fp32, bf16, i32 = mybir.dt.float32, mybir.dt.bfloat16, mybir.dt.int32
    ALU, ACT, AX = mybir.AluOpType, mybir.ActivationFunctionType, mybir.AxisListType

    N, D = x.shape
    H = w0.shape[0]
    P = 128
    NT = N // P
    CH = N // 2
    NK = CH // P
    VW = D + 1
    RING = 8
    PER_BANK = 512 // VW
    NB = -(-NK // PER_BANK)
    STAGE = 5
    T_AT, DEN_AT = 8, 7
    PER_LATE = 36
    WARM = 20
    WARM_FIRST = 28
    WARM_START = (16, 14)
    WARM_SHORT = 4
    ALPHA, EPS = 0.2, 1e-5
    U1, U2 = 2 * H, 2 * H + 2

    ctx = ExitStack()
    with ctx:
        def sb(name, shape, dt=fp32):
            return ctx.enter_context(nc.sbuf_tensor(name, shape, dt))

        def sem(name):
            return ctx.enter_context(nc.semaphore(name))

        adjT = sb("adjT", [P, NT, N], bf16)
        stage = sb("stage", [P, STAGE, CH], i32)
        probs = sb("probs", [P, RING, CH])
        rho = sb("rho", [P, N])
        rho_rows = sb("rho_rows", [H, N])
        V = sb("V", [P, NT, VW])
        X = sb("X", [P, NT, D])
        hT = sb("hT", [P, N])
        rows = sb("rows", [P, 2, NK, D])
        xn = sb("xn", [P, NK, D])
        fill = sb("fill", [P, NK, D])
        hpT = sb("hpT", [P, NK, P])
        W0 = sb("W0", [P, H, D])
        Wout = sb("Wout", [P, H, D])
        WL = sb("WL", [P, 3, VW])
        W0t = sb("W0t", [P, H, D])
        WLt = sb("WLt", [P, 3, D])
        a0_sb = sb("a0_sb", [P, H, 2])
        aL_sb = sb("aL_sb", [P, 3, 2])
        wa0 = sb("wa0", [P, 2, H])
        waL = sb("waL", [P, 4, 2])
        wa_now = sb("wa_now", [P, 2])
        bias_rep = sb("bias_rep", [P, D])
        mean_w = sb("mean_w", [P, H * D])
        mean_now = sb("mean_now", [P, D])
        ident = sb("ident", [P, P])
        stats = sb("stats", [P, NT, 6])
        mv = sb("mv", [P, NT, 2])
        nwt = sb("nwt", [P, 4, NT])
        seed = sb("seed", [P, NT], i32)
        hsum = sb("hsum", [P, 4])
        hmean = sb("hmean", [P, 2])
        cmax = sb("cmax", [P, H])
        s2_col = sb("s2_col", [P, NT])
        c_row = sb("c_row", [H, 1])
        c_rep = sb("c_rep", [P, H])
        d_all = sb("d_all", [P, H, NT])
        t_all = sb("t_all", [P, H, NT])
        v_all = sb("v_all", [P, H, NT])
        t_now = sb("t_now", [P, NT])
        v_now = sb("v_now", [P, NT])
        den = sb("den", [P, 4, NK])
        empty = sb("empty", [P, 2, NK])
        rho_dram = nc.dram_tensor("rho_dram", (H, N), fp32, kind="Internal").ap()

        acc = ctx.enter_context(nc.psum_tensor("acc", [P, 2, NB, 512], fp32))
        side = ctx.enter_context(nc.psum_tensor("side", [P, 2, 512], fp32))
        score_bank = acc[:, 0, 2, :]
        CT, CC, CW = 260, 390, 480
        idle = score_bank[:, CT:CT + P]
        idle_first = acc[:, 1, 2, 0:P]
        s1_banks = [acc[:, 0, 0, :], acc[:, 0, 1, :], acc[:, 1, 0, :], acc[:, 1, 1, :]]

        x_in = [sem(f"x_in{c}") for c in range(2)]
        w0_in = sem("w0_in")
        w0t_in = sem("w0t_in")
        w_in = sem("w_in")
        adj_in = [sem(f"adj_in{s}") for s in range(STAGE)]
        ident_zero = sem("ident_zero")
        ident_ready = sem("ident_ready")
        adj_ready = sem("adj_ready")
        wa_ready = sem("wa_ready")
        dve_step = sem("dve_step")
        wa_psum = sem("wa_psum")
        waL_psum = sem("waL_psum")
        waL_ready = sem("waL_ready")
        rstd_ready = sem("rstd_ready")
        norm_dve = sem("norm_dve")
        norm_act = sem("norm_act")
        hT_psum = sem("hT_psum")
        hT_ready = sem("hT_ready")
        s2_psum = sem("s2_psum")
        cmax_ready = sem("cmax_ready")
        cmaxT_psum = sem("cmaxT_psum")
        c_row_ready = sem("c_row_ready")
        c_psum = sem("c_psum")
        d_ready = sem("d_ready")
        tv_ready = sem("tv_ready")
        s1_psum = sem("s1_psum")
        r_ready = sem("r_ready")
        rho_ready = sem("rho_ready")
        rho_psum = sem("rho_psum")
        rho_stored = sem("rho_stored")
        rho_in = [sem(f"rho_in{c}") for c in range(2)]
        hmean_ready = sem("hmean_ready")
        meanw_psum = sem("meanw_psum")
        meanw_ready = sem("meanw_ready")
        mean_now_ready = sem("mean_now_ready")
        wh_psum = sem("wh_psum")
        wh_copied = sem("wh_copied")
        s1_copied = sem("s1_copied")
        v_ready = sem("v_ready")
        probs_ready = sem("probs_ready")
        summed = sem("summed")
        rden_ready = sem("rden_ready")
        fill_ready = sem("fill_ready")
        rows_ready = sem("rows_ready")
        act_ready = sem("act_ready")
        elu_ready = sem("elu_ready")
        hpT_psum = sem("hpT_psum")
        hpT_ready = sem("hpT_ready")
        proj_psum = sem("proj_psum")
        x_added = sem("x_added")
        x_written = sem("x_written")
        out_done = sem("out_done")

        block = ctx.enter_context(nc.Block())
        x_v = x.rearrange("(t p) d -> p t d", p=P)
        out_v = out.rearrange("(t p) d -> p t d", p=P)

        def group(c, k):
            return acc[:, c, k // PER_BANK, (k % PER_BANK) * VW:(k % PER_BANK) * VW + VW]

        def first_norm(n):
            return isinstance(n, int) and n == 0

        @block.sync
        def _(sp):
            for c in range(2):
                sp.dma_start(X[:, c * NK:(c + 1) * NK, :], x_v[:, c * NK:(c + 1) * NK, :]).then_inc(x_in[c], 16)
            sp.dma_start(W0t[:, :, :], w0_t.rearrange("h d f -> d h f")).then_inc(w0t_in, 16)
            sp.dma_start(a0_sb[:, :, :], a0).then_inc(w0t_in, 16)
            sp.dma_start(W0[:, :, :], w0.rearrange("h f d -> f h d")).then_inc(w0_in, 16)
            for n in range(2 * NT):
                c, j = n // NT, n % NT
                if n >= STAGE:
                    sp.wait_ge(adj_ready, n - STAGE + 1)
                sp.dma_start(stage[:, n % STAGE, :], adj_t[j * P:(j + 1) * P, c * CH:(c + 1) * CH]).then_inc(adj_in[n % STAGE], 16)
            sp.wait_ge(x_written, 10)
            sp.dma_start(out_v[:, 0:NK, :], X[:, 0:NK, :]).then_inc(out_done, 16)
            sp.wait_ge(x_written, 12)
            sp.dma_start(out_v[:, NK:NT, :], X[:, NK:NT, :]).then_inc(out_done, 16)
            sp.wait_ge(out_done, 32)

        @block.gpsimd
        def _(pool):
            nc.gpsimd.memset(ident[:, :], 0.0).then_inc(ident_zero, 1)
            pool.wait_ge(ident_zero, 1)
            nc.gpsimd.affine_select(out=ident[:, :], in_=ident[:, :], compare_op=ALU.not_equal, fill=1.0,
                                    base=0, pattern=[[-1, P]], channel_multiplier=1).then_inc(ident_ready, 1)
            for l, w in enumerate((w1_t, w2, w3)):
                pool.dma_start(WL[:, l, 0:D], w).then_inc(w_in, 16)
            for l, w in enumerate((w1, w2_t, w3_t)):
                pool.dma_start(WLt[:, l, :], w).then_inc(w_in, 16)
            for l, a in enumerate((r1, av2, av3)):
                pool.dma_start(aL_sb[:, l, :], a).then_inc(w_in, 16)
            pool.dma_start(bias_rep[:, :], b_out.rearrange("(o d) -> o d", o=1).to_broadcast([P, D])).then_inc(w_in, 16)
            pool.dma_start(Wout[:, :, :], w_out.rearrange("(h d) o -> d h o", h=H)).then_inc(w_in, 16)

            def load_rho(h, c):
                pool.dma_start(rho[:, c * CH:(c + 1) * CH],
                               rho_dram[bass.ds(h, 1), c * CH:(c + 1) * CH].to_broadcast([P, CH])).then_inc(rho_in[c], 16)

            for c in range(2):
                pool.wait_ge(rho_ready, 2 * c + 2)
                pool.dma_start(rho_dram[:, c * CH:(c + 1) * CH], rho_rows[:, c * CH:(c + 1) * CH]).then_inc(rho_stored, 16)
                pool.wait_ge(rho_stored, 16 * c + 16)
                if c == 1:
                    load_rho(0, c)
            with pool.Fori(0, H - 1) as h:
                for c in range(2):
                    pool.wait_ge(probs_ready, h * (2 * NT) + (c + 1) * NT)
                    load_rho(h + 1, c)

        @block.tensor
        def _(pe):
            def transpose_normed(n, c):
                for r in range(2 * c, 2 * c + 2):
                    pe.wait_ge(norm_act if r % 2 else norm_dve, 2 * n + c + 1)
                    for k in range(4):
                        last = nc.tensor.transpose(side[:, r % 2, k * P:(k + 1) * P],
                                                   xn[:, (r % 2) * 4 + k, :], ident[:, :])
                    last.then_inc(hT_psum, 1)
                if first_norm(n) or c == 1:
                    keep_warm(WARM_SHORT, idle_first if first_norm(n) else idle)
                pe.wait_ge(hT_ready, n * 4 + 2 * c + 2)
                if c == 0:
                    pe.wait_ge(wa_ready, n + 1)

            def s2_of_heads(c):
                for j in range(c * NK, (c + 1) * NK):
                    last = nc.tensor.matmul(score_bank[:, j * H:(j + 1) * H], hT[:, j * P:(j + 1) * P],
                                            wa0[:, 1, :], start=True, stop=True)
                last.then_inc(s2_psum, 1)

            def wh_and_s2(c, w):
                for k in range(NK):
                    at = (c * NK + k) * P
                    last = nc.tensor.matmul(group(c, k), hT[:, at:at + P], w, start=True, stop=True)
                last.then_inc(s2_psum, 1)

            def s1(k, wa_s1, bank):
                nc.tensor.matmul(bank[0:wa_s1.shape[1], :], wa_s1, hT[:, k * 512:(k + 1) * 512],
                                 start=True, stop=True).then_inc(s1_psum, 1)

            def project(q, g, w, before=None):
                if g >= 2:
                    pe.wait_ge(v_ready, q * 4 + g - 1)
                elif before is not None:
                    pe.wait_ge(x_added, before + g)
                for k in range(4):
                    j = 4 * g + k
                    last = nc.tensor.matmul(side[:, g % 2, k * D:(k + 1) * D], hT[:, j * P:(j + 1) * P], w,
                                            start=True, stop=True)
                last.then_inc(wh_psum, 1)

            def spread_max(n, heads):
                pe.wait_ge(cmax_ready, n + 1)
                nc.tensor.transpose(score_bank[0:heads, CT:CT + P], cmax[:, 0:heads], ident[:, :]).then_inc(cmaxT_psum, 1)
                pe.wait_ge(c_row_ready, n + 1)
                nc.tensor.matmul(score_bank[:, CC:CC + heads], c_row[0:heads, 0:1].to_broadcast([heads, P]),
                                 ident[0:heads, 0:heads], start=True, stop=True).then_inc(c_psum, 1)

            def early_scores(n, wa_s1, w):
                wh_and_s2(0, w)
                s1(0, wa_s1, side[:, 0, :])
                s1(1, wa_s1, side[:, 1, :])

            def keep_warm(count, where):
                for k in range(count):
                    nc.tensor.matmul(where, ident[:, :], ident[:, :], start=True, stop=True)

            def late_scores(n, wa_s1, w):
                pe.wait_ge(s1_copied, 2 * n)
                transpose_normed(n, 1)
                wh_and_s2(1, w)
                spread_max(n, 1)
                s1(2, wa_s1, side[:, 0, :])
                s1(3, wa_s1, side[:, 1, :])

            def rest_of_wh(q, w):
                return ((1, lambda: project(q, 2, w)), (3, lambda: project(q, 3, w)))

            def mean_rows(m, w, heads, sem_free, value):
                pe.wait_ge(hmean_ready, m)
                pe.wait_ge(sem_free, value)
                cols = min(512, heads * D)
                for k in range(heads * D // cols):
                    last = nc.tensor.matmul(side[:, k, 0:cols], hmean[:, 1:2].to_broadcast([P, P]),
                                            w[:, k * cols:(k + 1) * cols], start=True, stop=True)
                last.then_inc(meanw_psum, 1)

            def unit(u, c, q, asides=(), later=None):
                if later is not None:
                    pe.wait_ge(wh_copied, 2 * later)
                for j in range(NT):
                    if j == 0 and not (isinstance(u, int) and u == 0):
                        pe.wait_ge(rows_ready, 2 * u - 1)
                    if c == 0 and j % 4 == 0:
                        pe.wait_ge(v_ready, q * 4 + j // 4 + 1)
                    pe.wait_ge(probs_ready, u * NT + j + 1)
                    for k in range(NK):
                        last = nc.tensor.matmul(group(c, k), probs[:, j % RING, k * P:(k + 1) * P], V[:, j, :],
                                                start=(j == 0 and k % PER_BANK == 0), stop=(j == NT - 1),
                                                skip_group_check=True)
                    last.then_inc(summed, 1)
                    for at, work in asides:
                        if at == j:
                            work()

            def transpose_rows(u, q):
                pe.wait_ge(elu_ready, u + 1)
                pe.wait_ge(x_added, 2 * u + 1)
                pe.wait_ge(v_ready, q * 4 + 4)
                for b in range(2):
                    for k in range(4):
                        last = nc.tensor.transpose(side[:, b, k * P:(k + 1) * P], rows[:, 0, 4 * b + k, :], ident[:, :])
                    last.then_inc(hpT_psum, 1)

            def out_projection(u, w):
                for b in range(2):
                    pe.wait_ge(hpT_ready, 2 * u + b + 1)
                    for k in range(4):
                        last = nc.tensor.matmul(side[:, b, k * D:(k + 1) * D], hpT[:, 4 * b + k, :], w,
                                                start=True, stop=True)
                    last.then_inc(proj_psum, 1)

            def aside(u, q, w):
                return ((T_AT, lambda: transpose_rows(u, q)), (T_AT + 2, lambda: out_projection(u, w)))

            def head_of(t, h):
                return t[:, bass.ds(h, 1), :].rearrange("p a d -> p (a d)")

            pe.wait_ge(ident_ready, 1)
            keep_warm(WARM_START[0], idle_first)
            pe.wait_ge(w0t_in, 32)
            for h in range(H):
                last = nc.tensor.matmul(score_bank[:, CW + 2 * h:CW + 2 * h + 2], W0t[:, h, :], a0_sb[:, h, :],
                                        start=True, stop=True)
            last.then_inc(wa_psum, 1)

            def later_vectors():
                pe.wait_ge(w_in, 11 * 16)
                pe.wait_ge(meanw_ready, 1)
                for l in range(3):
                    last = nc.tensor.matmul(side[:, 0, 2 * l:2 * l + 2], WLt[:, l, :], aL_sb[:, l, :], start=True, stop=True)
                last.then_inc(waL_psum, 1)

            keep_warm(WARM_START[1], idle_first)
            wa1 = wa0[:, 0, :]
            for c in range(2):
                transpose_normed(0, c)
                s2_of_heads(c)
            spread_max(0, H)
            s1(0, wa1, s1_banks[0])
            s1(1, wa1, s1_banks[1])
            pe.wait_ge(w0_in, 16)
            project(0, 0, W0[:, 0, :])
            for k in range(2):
                pe.wait_ge(rho_ready, k + 1)
                nc.tensor.matmul(s1_banks[k], ident[0:H, 0:1].to_broadcast([H, P]), rho_rows[:, k * 512:(k + 1) * 512],
                                 start=True, stop=True).then_inc(rho_psum, 1)
            project(0, 1, W0[:, 0, :])
            unit(0, 0, 0, ((0, lambda: (s1(2, wa1, s1_banks[2]), s1(3, wa1, s1_banks[3]))),) + rest_of_wh(0, W0[:, 0, :]) + (
                (7, lambda: mean_rows(1, W0[:, :, :].rearrange("p h d -> p (h d)"), H, v_ready, 4)),
                (13, later_vectors)))
            pe.wait_ge(waL_ready, 1)
            pe.wait_ge(r_ready, 4)
            with pe.Fori(0, H - 1) as h:
                w = head_of(W0, h + 1)
                unit(2 * h + 1, 1, h, aside(2 * h, h, head_of(Wout, h)) + (
                    (11, lambda: project(h + 1, 0, w, before=4 * h + 2)),
                    (12, lambda: project(h + 1, 1, w, before=4 * h + 2)),
                    (14, lambda: project(h + 1, 2, w))))
                project(h + 1, 3, w)
                unit(2 * h + 2, 0, h + 1, aside(2 * h + 1, h + 1, head_of(Wout, h)))
            unit(2 * H - 1, 1, H - 1, aside(2 * H - 2, H - 1, Wout[:, H - 1, :]))

            wa1 = wa_now[:, 0:1].to_broadcast([P, P])
            pe.wait_ge(x_added, 4 * H - 1)
            transpose_normed(1, 0)
            early_scores(1, wa1, WL[:, 0, :])
            pe.wait_ge(s1_copied, 2)
            transpose_rows(2 * H - 1, H - 1)
            out_projection(2 * H - 1, Wout[:, H - 1, :])
            pe.wait_ge(wh_copied, 1)
            keep_warm(WARM_FIRST, idle)
            late_scores(1, wa1, WL[:, 0, :])
            unit(U1, 0, H, later=1)
            unit(U1 + 1, 1, H)
            transpose_normed(2, 0)
            with pe.Fori(0, 2) as l:
                w = head_of(WL, l + 1)
                early_scores(l + 2, wa1, w)
                pe.wait_ge(wh_copied, 2 * l + 3)
                keep_warm(WARM, idle)
                late_scores(l + 2, wa1, w)
                unit(2 * l + U2, 0, l + (H + 1), ((7, lambda: mean_rows(l + 2, w[:, 0:D], 1, r_ready, l * 4 + 12)),),
                     later=l + 2)
                unit(2 * l + (U2 + 1), 1, l + (H + 1))
                pe.wait_ge(meanw_ready, l + 2)
                transpose_normed(l + 3, 0)

        @block.scalar
        def _(act):
            def cast(n0, n1):
                for n in range(n0, n1):
                    c, j = n // NT, n % NT
                    act.wait_ge(adj_in[n % STAGE], 16 * (n // STAGE + 1))
                    nc.scalar.activation(adjT[:, j, c * CH:(c + 1) * CH], stage[:, n % STAGE, :], ACT.Sign).then_inc(adj_ready, 1)

            def relu_transposed(n, c):
                act.wait_ge(rstd_ready, n + 1 if first_norm(n) else 2 * n + c)
                for k in range(4, NK):
                    at = c * NK + k
                    last = nc.scalar.activation(xn[:, k, :], X[:, at, :], ACT.Identity, bias=nwt[:, 3, at:at + 1],
                                                scale=nwt[:, 0, at:at + 1])
                last.then_inc(norm_act, 1)
                for r in range(2 * c, 2 * c + 2):
                    act.wait_ge(hT_psum, n * 4 + r + 1)
                    nc.scalar.activation(hT[:, r * 512:(r + 1) * 512], side[:, r % 2, :], ACT.Relu,
                                         accum_out=hsum[:, r:r + 1]).then_inc(hT_ready, 1)

            def factors(n, heads):
                act.wait_ge(d_ready, n + 1)
                t_out = t_all[:, :, :] if heads > 1 else t_now[:, :]
                v_out = v_all[:, :, :] if heads > 1 else v_now[:, :]
                d_in = d_all[:, :, :] if heads > 1 else d_all[:, 0, :]
                nc.scalar.activation(t_out, d_in, ACT.Exp, scale=1 - ALPHA).then_inc(tv_ready, 1)
                nc.scalar.activation(v_out, d_in, ACT.Exp, scale=ALPHA).then_inc(tv_ready, 1)

            def rho_exp(n, c, heads):
                r_buf = rho_rows if heads > 1 else rho
                for k in range(2 * c, 2 * c + 2):
                    act.wait_ge(r_ready, n * 4 + k + 1)
                    nc.scalar.activation(r_buf[:, k * 512:(k + 1) * 512], r_buf[:, k * 512:(k + 1) * 512], ACT.Exp,
                                         scale=-(1 - ALPHA)).then_inc(rho_ready, 1)

            def scale_v(q, between=None):
                for g in range(4):
                    act.wait_ge(wh_psum, q * 4 + g + 1)
                    nc.scalar.activation(V[:, 4 * g:4 * g + 4, D], v_now[:, 4 * g:4 * g + 4], ACT.Copy)
                    for k in range(4):
                        last = nc.scalar.activation(V[:, 4 * g + k, 0:D], side[:, g % 2, k * D:(k + 1) * D], ACT.Copy,
                                                    scale=v_now[:, 4 * g + k:4 * g + k + 1])
                    last.then_inc(v_ready, 1)
                    if between is not None:
                        between(g)

            def copy_wh(n, c):
                if c == 0:
                    act.wait_ge(s2_psum, 2 * n + 1)
                else:
                    act.wait_ge(cmax_ready, n + 1)
                for b in range(NB):
                    m = min(PER_BANK, NK - b * PER_BANK)
                    last = nc.scalar.activation(V[:, c * NK + b * PER_BANK:c * NK + b * PER_BANK + m, :],
                                                acc[:, c, b, 0:m * VW].rearrange("p (k v) -> p k v", k=m), ACT.Copy)
                last.then_inc(wh_copied, 1)

            def copy_early(n):
                copy_wh(n, 0)
                for k in range(2):
                    act.wait_ge(s1_psum, n * 4 + k + 1)
                    nc.scalar.activation(rho[:, k * 512:(k + 1) * 512], side[:, k, :], ACT.Copy).then_inc(s1_copied, 1)

            def scale_v_later(n, groups):
                for g in groups:
                    nc.scalar.activation(V[:, 4 * g:4 * g + 4, D], v_now[:, 4 * g:4 * g + 4], ACT.Copy)
                    for k in range(4 * g, 4 * g + 4):
                        last = nc.scalar.activation(V[:, k, 0:D], V[:, k, 0:D], ACT.Copy, scale=v_now[:, k:k + 1])
                    last.then_inc(v_ready, 1)

            def copy_mean(m, heads):
                act.wait_ge(meanw_psum, m)
                cols = min(512, heads * D)
                for k in range(heads * D // cols):
                    last = nc.scalar.activation(mean_w[:, k * cols:(k + 1) * cols], side[:, k, 0:cols], ACT.Copy)
                last.then_inc(meanw_ready, 1)
                act.wait_ge(meanw_ready, m)

            def take_mean(w, count):
                nc.scalar.activation(mean_now[:, :], w, ACT.Copy).then_inc(mean_now_ready, 1)
                act.wait_ge(mean_now_ready, count)

            def fill_rows(c):
                for k in range(NK):
                    ins = nc.scalar.activation(fill[:, k, :], mean_now[:, :], ACT.Copy, scale=empty[:, c, k:k + 1])
                    if k % 4 == 3:
                        ins.then_inc(fill_ready, 1)

            def nonlinear(u, func):
                for b in range(2):
                    act.wait_ge(rows_ready, 2 * u + b + 2)
                    nc.scalar.activation(rows[:, 1, 4 * b:4 * b + 4, :], rows[:, 0, 4 * b:4 * b + 4, :],
                                         func).then_inc(act_ready, 1)

            def copy_transposed(u):
                for b in range(2):
                    act.wait_ge(hpT_psum, 2 * u + b + 1)
                    nc.scalar.activation(hpT[:, 4 * b:4 * b + 4, :], side[:, b, :].rearrange("p (k i) -> p k i", k=4),
                                         ACT.Copy).then_inc(hpT_ready, 1)

            def finish(u, c):
                act.wait_ge(rden_ready, u + 1)
                fill_rows(c)
                nonlinear(u, ACT.Exp)
                copy_transposed(u)

            act.wait_ge(wa_psum, 1)
            nc.scalar.activation(wa0[:, :, :], score_bank[:, CW:CW + 2 * H].rearrange("p (h s) -> p s h", s=2),
                                 ACT.Copy).then_inc(wa_ready, 1)
            relu_transposed(0, 0)
            relu_transposed(0, 1)
            cast(0, 6)
            factors(0, H)
            rho_exp(0, 0, H)
            act.wait_ge(tv_ready, 2)
            nc.scalar.activation(v_now[:, :], v_all[:, 0, :], ACT.Copy).then_inc(tv_ready, 1)
            act.wait_ge(tv_ready, 3)
            scale_v(0, lambda g: (cast(6 + 3 * g, 9 + 3 * g), g == 1 and rho_exp(0, 1, H)))
            copy_mean(1, H)
            take_mean(mean_w[:, 0:D], 1)
            cast(18, 24)
            act.wait_ge(waL_psum, 1)
            nc.scalar.activation(WL[:, 0:3, D], side[:, 0, 1:6:2], ACT.Copy)
            nc.scalar.activation(waL[:, 0:3, :], side[:, 0, 0:6].rearrange("p (l s) -> p l s", l=3), ACT.Copy).then_inc(waL_ready, 1)
            cast(24, 2 * NT)
            with act.Fori(0, H - 1) as h:
                finish(2 * h, 0)
                nc.scalar.activation(v_now[:, :], v_all[:, bass.ds(h + 1, 1), :].rearrange("p a t -> p (a t)"),
                                     ACT.Copy).then_inc(tv_ready, 1)
                act.wait_ge(tv_ready, h + 4)
                scale_v(h + 1)
                finish(2 * h + 1, 1)
                take_mean(mean_w[:, bass.ds((h + 1) * D, D)], h + 2)
            finish(2 * H - 2, 0)
            fill_rows(1)
            relu_transposed(1, 0)
            nonlinear(2 * H - 1, ACT.Exp)
            copy_early(1)
            copy_transposed(2 * H - 1)

            def start_layer(n, tv):
                relu_transposed(n, 1)
                copy_wh(n, 1)
                factors(n, 1)
                rho_exp(n, 0, 1)
                act.wait_ge(wh_copied, 2 * n)
                act.wait_ge(tv_ready, tv)
                scale_v_later(n, range(4))
                rho_exp(n, 1, 1)

            start_layer(1, H + 4)
            nonlinear(U1, ACT.Gelu)
            relu_transposed(2, 0)
            nonlinear(U1 + 1, ACT.Gelu)
            with act.Fori(0, 2) as l:
                copy_early(l + 2)
                start_layer(l + 2, 2 * l + (H + 6))
                copy_mean(l + 2, 1)
                take_mean(mean_w[:, 0:D], l + (H + 1))
                fill_rows(0)
                nonlinear(2 * l + U2, ACT.Exp)
                fill_rows(1)
                relu_transposed(l + 3, 0)
                nonlinear(2 * l + (U2 + 1), ACT.Exp)

        @block.vector
        def _(dve):
            steps = [0]
            base = [0]

            def link(ins):
                steps[0] += 1
                ins.then_inc(dve_step, 1)
                dve.wait_ge(dve_step, base[0] + steps[0])

            def norm(n, halves, last_added=None):
                first, end = halves[0] * NK, (halves[-1] + 1) * NK
                for k in range(first, end):
                    if first_norm(n) and k % NK == 0:
                        dve.wait_ge(x_in[k // NK], 16)
                    elif isinstance(n, int) and n == 1:
                        if k == first:
                            dve.wait_ge(dve_step, last_added)
                    elif not first_norm(n) and k % 4 == 0:
                        dve.wait_ge(x_written, (n - 2) * 4 + k // 4 + 1)
                    last = nc.vector.bn_stats(stats[:, k, :], X[:, k, :])
                link(last)
                nc.vector.memset(nwt[:, 2, first:end], 0.0)
                for k in range(first, end):
                    last = nc.vector.bn_aggr(mv[:, k, :], stats[:, k, :])
                link(last)
                y, v, s, m = (nwt[:, i, first:end] for i in range(4))
                link(nc.vector.tensor_scalar(v, mv[:, first:end, 1], EPS, None, ALU.add))
                link(nc.vector.tensor_scalar(seed[:, first:end], v.bitcast(i32), -0.5, 1597463007.0, ALU.mult, ALU.add))
                g = seed[:, first:end].bitcast(fp32)
                for it in range(3):
                    link(nc.vector.scalar_tensor_tensor(s, g, -0.5, g, ALU.mult, ALU.mult))
                    link(nc.vector.tensor_tensor(s, s, v, ALU.mult))
                    link(nc.vector.scalar_tensor_tensor(y, s, 1.5, g, ALU.add, ALU.mult))
                    g = y
                nc.vector.scalar_tensor_tensor(m, mv[:, first:end, 0], -1.0, y, ALU.mult, ALU.mult).then_inc(rstd_ready, 1)
                for c in halves:
                    if c == 1 or not first_norm(n):
                        dve.wait_ge(hT_psum, n * 4 + 2 * c)
                    for k in range(4):
                        at = c * NK + k
                        ins = nc.vector.tensor_scalar(xn[:, k, :], X[:, at, :], mv[:, at, 0:1], nwt[:, 0, at:at + 1],
                                                      ALU.subtract, ALU.mult)
                    ins.then_inc(norm_dve, 1)

            def last_columns(to, c):
                full = NK // PER_BANK
                nc.vector.tensor_copy(to[:, 0:full * PER_BANK].rearrange("p (b g) -> p b g", g=PER_BANK),
                                      acc[:, c, 0:full, D:D + PER_BANK * VW - D:VW])
                link(nc.vector.tensor_copy(to[:, full * PER_BANK:NK],
                                           acc[:, c, full, D:D + (NK - full * PER_BANK - 1) * VW + 1:VW]))

            def center(n, heads):
                if heads == 1:
                    dve.wait_ge(wh_copied, 2 * n - 1)
                    nc.vector.tensor_copy(s2_col[:, 0:NK], V[:, 0:NK, D])
                dve.wait_ge(s2_psum, 2 * n + 2)
                if heads > 1:
                    s2 = score_bank[:, 0:NT * heads].rearrange("p (t h) -> p h t", h=heads)
                else:
                    last_columns(s2_col[:, NK:NT], 1)
                    s2 = s2_col[:, :]
                nc.vector.tensor_reduce(cmax[:, 0:heads], s2, AX.X, ALU.max).then_inc(cmax_ready, 1)
                dve.wait_ge(cmaxT_psum, n + 1)
                nc.vector.tensor_reduce(c_row[0:heads, :], score_bank[0:heads, CT:CT + P], AX.X, ALU.max).then_inc(c_row_ready, 1)
                dve.wait_ge(c_psum, n + 1)
                link(nc.vector.tensor_copy(c_rep[:, 0:heads], score_bank[:, CC:CC + heads]))
                for k in range(heads):
                    last = nc.vector.tensor_scalar(d_all[:, k, :], s2[:, k, :] if heads > 1 else s2, c_rep[:, k:k + 1],
                                                   None, ALU.subtract)
                last.then_inc(d_ready, 1)

            def mean(n, m):
                dve.wait_ge(hT_ready, n * 4 + 4)
                link(nc.vector.tensor_reduce(hmean[:, 0:1], hsum[:, :], AX.X, ALU.add))
                nc.vector.tensor_scalar(hmean[:, 1:2], hmean[:, 0:1], 1.0 / N, None, ALU.mult).then_inc(hmean_ready, 1)

            def r_rows(n, c, heads):
                r_buf, c_s, m = (rho_rows, c_row, heads) if heads > 1 else (rho, c_rep, P)
                for k in range(2 * c, 2 * c + 2):
                    to = r_buf[0:m, k * 512:(k + 1) * 512]
                    if heads == 1 and c == 0:
                        dve.wait_ge(s1_copied, n * 2 + k - 1)
                        s1_rows = to
                    else:
                        dve.wait_ge(s1_psum, n * 4 + k + 1)
                        s1_rows = s1_banks[k][0:m, :] if heads > 1 else side[:, k % 2, :]
                    nc.vector.tensor_scalar(to, s1_rows, c_s[0:m, 0:1], 0.0, ALU.add, ALU.max).then_inc(r_ready, 1)

            def unit(u, c, before=None, asides=()):
                for j in range(NT):
                    if before is not None:
                        before(j)
                    if not (isinstance(u, int) and u * NT + j < RING):
                        dve.wait_ge(summed, u * NT + j - RING + 1)
                    nc.vector.scalar_tensor_tensor(probs[:, j % RING, :], rho[:, c * CH:(c + 1) * CH], t_now[:, j:j + 1],
                                                   adjT[:, j, c * CH:(c + 1) * CH], ALU.max, ALU.mult).then_inc(probs_ready, 1)
                    for at, work in asides:
                        if at == j:
                            work()

            def denominators(u, c, guard=True, store=False):
                dve.wait_ge(summed, (u + 1) * NT)
                last_columns(den[:, 0, :], c)
                if store:
                    nc.vector.tensor_scalar(empty[:, c, :], den[:, 0, :], 0.0, None, ALU.is_equal)
                if guard:
                    link(nc.vector.scalar_tensor_tensor(den[:, 2, :], den[:, 0, :], 0.0, den[:, 0, :], ALU.is_equal, ALU.add))
                nc.vector.reciprocal(den[:, 3, :], den[:, 2 if guard else 0, :]).then_inc(rden_ready, 1)
                dve.wait_ge(rden_ready, u + 1)

            def divide(u, c, f):
                for k in range(NK):
                    if f is not None:
                        if k % 4 == 0:
                            dve.wait_ge(fill_ready, 2 * f + k // 4 + 1)
                        ins = nc.vector.scalar_tensor_tensor(rows[:, 0, k, :], group(c, k)[:, 0:D], den[:, 3, k:k + 1],
                                                             fill[:, k, :], ALU.mult, ALU.add)
                    else:
                        ins = nc.vector.tensor_scalar(rows[:, 0, k, :], group(c, k)[:, 0:D], den[:, 3, k:k + 1], None, ALU.mult)
                    if k % 4 == 3:
                        ins.then_inc(rows_ready, 1)

            def elu(u):
                dve.wait_ge(act_ready, 2 * u + 2)
                link(nc.vector.tensor_scalar(rows[:, 1, :, :], rows[:, 1, :, :], 1.0, 1.0, ALU.min, ALU.subtract))
                nc.vector.scalar_tensor_tensor(rows[:, 0, :, :], rows[:, 0, :, :], 0.0, rows[:, 1, :, :],
                                               ALU.max, ALU.add).then_inc(elu_ready, 1)

            def add_projection(u, c):
                for b in range(2):
                    dve.wait_ge(proj_psum, 2 * u + b + 1)
                    at = X[:, c * NK + 4 * b:c * NK + 4 * b + 4, :]
                    nc.vector.tensor_tensor(at, at, side[:, b, :].rearrange("p (k d) -> p k d", k=4), ALU.add).then_inc(x_added, 1)

            def head0_asides(u, c, store=True):
                return ((DEN_AT, lambda: denominators(u, c, store=store)),
                        (DEN_AT + 2, lambda: divide(u, c, u)),
                        (DEN_AT + 4, lambda: elu(u)),
                        (15, lambda: add_projection(u, c)))

            def add_elu(u, c):
                at = [X[:, c * NK + 4 * b:c * NK + 4 * b + 4, :] for b in range(2)]
                for b in range(2):
                    dve.wait_ge(rows_ready, 2 * u + b + 2)
                    last = nc.vector.scalar_tensor_tensor(at[b], rows[:, 0, 4 * b:4 * b + 4, :], 0.0, at[b], ALU.max, ALU.add)
                link(last)
                for b in range(2):
                    dve.wait_ge(act_ready, 2 * u + b + 1)
                    nc.vector.scalar_tensor_tensor(at[b], rows[:, 1, 4 * b:4 * b + 4, :], 1.0, at[b],
                                                   ALU.min, ALU.add).then_inc(x_written, 1)

            def add_gelu(u, c):
                for b in range(2):
                    at = X[:, c * NK + 4 * b:c * NK + 4 * b + 4, :]
                    dve.wait_ge(act_ready, 2 * u + b + 1)
                    nc.vector.tensor_tensor(at, at, rows[:, 1, 4 * b:4 * b + 4, :], ALU.add).then_inc(x_written, 1)

            norm(0, (0, 1))
            center(0, H)
            r_rows(0, 0, H)
            dve.wait_ge(tv_ready, 1)
            nc.vector.tensor_copy(t_now[:, :], t_all[:, 0, :]).then_inc(rows_ready, 1)
            dve.wait_ge(rows_ready, 1)
            for k in range(2):
                dve.wait_ge(rho_psum, k + 1)
                last = nc.vector.tensor_copy(rho[:, k * 512:(k + 1) * 512], s1_banks[k])
            link(last)

            def rho_and_adj(h, c, blocks):
                def before(j):
                    if j == 0 and c == 1:
                        dve.wait_ge(rho_in[1], (h + 1) * 16)
                    elif j == 0 and not isinstance(h, int):
                        dve.wait_ge(rho_in[0], h * 16)
                    if blocks:
                        dve.wait_ge(adj_ready, c * NT + j + 1)
                return before

            def add_bias():
                dve.wait_ge(w_in, 11 * 16)
                link(nc.vector.memset(waL[:, 3, :], 0.0))
                nc.vector.tensor_tensor(X[:, :, :], X[:, :, :], bias_rep[:, :].rearrange("p (a d) -> p a d", a=1)
                                        .to_broadcast([P, NT, D]), ALU.add).then_inc(x_added, 1)
                dve.wait_ge(x_added, 1)

            unit(0, 0, rho_and_adj(0, 0, True), ((3, lambda: r_rows(0, 1, H)), (4, lambda: mean(0, 1)), (8, add_bias)))
            PER = 1 + 2 * 3
            outside, steps[0] = steps[0], 0
            with dve.Fori(0, H - 1) as h:
                base[0] = h * PER + outside
                unit(2 * h + 1, 1, rho_and_adj(h, 1, True), head0_asides(2 * h, 0))
                dve.wait_ge(probs_ready, (2 * h + 2) * NT)
                link(nc.vector.tensor_copy(t_now[:, :], t_all[:, bass.ds(h + 1, 1), :].rearrange("p a t -> p (a t)")))
                unit(2 * h + 2, 0, rho_and_adj(h + 1, 0, False), head0_asides(2 * h + 1, 1))
                assert steps[0] == PER, steps[0]
            base[0] = 0
            steps[0] = outside + (H - 1) * PER
            unit(2 * H - 1, 1, rho_and_adj(H - 1, 1, False), head0_asides(2 * H - 2, 0))
            dve.wait_ge(waL_ready, 1)
            nc.vector.tensor_copy(wa_now[:, :], waL[:, 0, :]).then_inc(wa_ready, 1)
            dve.wait_ge(x_added, 4 * H - 1)
            last_link = base[0] + steps[0]
            norm(1, (0,), last_link)
            for _, work in head0_asides(2 * H - 1, 1, store=False):
                work()
            dve.wait_ge(x_added, 4 * H + 1)
            last_link = base[0] + steps[0]
            norm(1, (1,), last_link)

            center(1, 1)
            r_rows(1, 0, 1)
            dve.wait_ge(tv_ready, H + 3)
            dve.wait_ge(rho_ready, 6)
            unit(U1, 0, None, ((5, lambda: r_rows(1, 1, 1)),))
            dve.wait_ge(rho_ready, 8)

            def next_attention_vectors(n, l):
                dve.wait_ge(s1_psum, n * 4 + 4)
                nc.vector.tensor_copy(wa_now[:, :], waL[:, bass.ds(l, 1), :].rearrange("p a s -> p (a s)")
                                      if not isinstance(l, int) else waL[:, l, :]).then_inc(wa_ready, 1)

            unit(U1 + 1, 1, None, ((DEN_AT, lambda: denominators(U1, 0, False)),
                                   (DEN_AT + 1, lambda: divide(U1, 0, None)),
                                   (DEN_AT + 4, lambda: add_gelu(U1, 0)),
                                   (15, lambda: (next_attention_vectors(1, 1), norm(2, (0,))))))
            denominators(U1 + 1, 1, False)
            divide(U1 + 1, 1, None)
            add_gelu(U1 + 1, 1)

            PER = PER_LATE
            outside, steps[0] = steps[0], 0
            with dve.Fori(0, 2) as l:
                base[0] = l * PER + outside
                n, u, f = l + 2, 2 * l + U2, 2 * l + 2 * H
                norm(n, (1,))
                center(n, 1)
                r_rows(n, 0, 1)
                dve.wait_ge(tv_ready, 2 * l + (H + 5))
                dve.wait_ge(rho_ready, 4 * l + 10)
                unit(u, 0, None, ((2, lambda: mean(n, n)),
                                  (5, lambda: r_rows(n, 1, 1)),
                                  (9, lambda: link(nc.vector.tensor_scalar(X[:, :, :], X[:, :, :], 1.0, None, ALU.subtract)))))
                dve.wait_ge(rho_ready, 4 * l + 12)

                unit(u + 1, 1, None, ((DEN_AT, lambda: denominators(u, 0)),
                                      (DEN_AT + 2, lambda: divide(u, 0, f)),
                                      (DEN_AT + 4, lambda: add_elu(u, 0)),
                                      (15, lambda: (next_attention_vectors(n, l + 2), norm(n + 1, (0,))))))
                denominators(u + 1, 1)
                divide(u + 1, 1, f + 1)
                add_elu(u + 1, 1)
                assert steps[0] == PER, steps[0]


_INS = ["x", "adj_t", "L0_gnn_W_heads", "W0_t", "a0", "L0_gnn_W_out", "L0_gnn_b_out", "W1_t", "L1_gnn_W", "r1",
        "L2_gnn_W", "W2_t", "a2", "L3_gnn_W", "W3_t", "a3"]


def kernel(**inputs):
    import numpy as _np
    import concourse.bacc as _bacc
    from concourse import mybir as _mybir
    from concourse.bass_utils import run_bass_kernel_spmd as _run

    laid = dict(inputs)
    laid["adj_t"] = _np.asarray(inputs["adj"]).T
    laid["W0_t"] = _np.asarray(inputs["L0_gnn_W_heads"]).transpose(0, 2, 1)
    laid["a0"] = _np.stack([_np.asarray(inputs["L0_gnn_a1"]), _np.asarray(inputs["L0_gnn_a2"])], axis=-1).transpose(1, 0, 2)
    laid["W1_t"] = _np.asarray(inputs["L1_gnn_W"]).T
    laid["W2_t"] = _np.asarray(inputs["L2_gnn_W"]).T
    laid["W3_t"] = _np.asarray(inputs["L3_gnn_W"]).T
    for to, name in (("r1", "L1_gnn_r"), ("a2", "L2_gnn_a"), ("a3", "L3_gnn_a")):
        laid[to] = _np.asarray(inputs[name]).reshape(2, -1).T
    nc = _bacc.Bacc("TRN2", target_bir_lowering=False, num_devices=1)
    arrays, args = {}, []
    for name in _INS:
        a = _np.ascontiguousarray(laid[name])
        arrays[f"in_{name}_dram"] = a
        args.append(nc.dram_tensor(f"in_{name}_dram", a.shape, _mybir.dt.from_np(a.dtype), kind="ExternalInput").ap())
    out = nc.dram_tensor("out_0_dram", inputs["x"].shape, _mybir.dt.float32, kind="ExternalOutput").ap()
    gat_stack(nc, *args, out)
    r = _run(nc, [arrays], core_ids=[0])
    return r.results[0]["out_0_dram"]
```
